# Optimizing a Trainium2 kernel written in Bass

```python
import numpy as np
import jax
import jax.numpy as jnp

def _softmax(x, axis=-1):
    return jax.nn.softmax(x, axis=axis)

def _gelu(x):
    return jax.nn.gelu(x, approximate=True)

def _silu(x):
    return jax.nn.silu(x)

def _sigmoid(x):
    return jax.nn.sigmoid(x)

def _layernorm(x, axis=-1, eps=1e-05):
    m = jnp.mean(x, axis=axis, keepdims=True)
    v = jnp.var(x, axis=axis, keepdims=True)
    return (x - m) / jnp.sqrt(v + eps)

def _scatter_add(tgt, idx, src, axis=0):
    return tgt.at[idx].add(src)

def _segment_sum(src, seg, n):
    return jax.ops.segment_sum(src, seg, n)
kernel_name = 'mk_hybrid_d1_jaxref_r4_208a9e'

def setup_inputs(seed: int=0):
    np.random.seed(seed)
    _w = jnp.asarray

    def _L0_attn_a_setup():
        import jax, jax.numpy as jnp
        import numpy as np
        H = 16
        WIN = 64
        key = jax.random.key(seed)
        k1, k2, k3, k4 = jax.random.split(key, 4)
        B, N, C = (2, 1024, 256)
        x = jax.random.normal(k1, (B, N, C), dtype=jnp.float32)
        w_qkv = jax.random.normal(k2, (C, 3 * C), dtype=jnp.float32) * 0.02
        w_proj = jax.random.normal(k3, (C, C), dtype=jnp.float32) * 0.02
        b_proj = jax.random.normal(k4, (C,), dtype=jnp.float32) * 0.02
        return {'x': x, 'w_qkv': w_qkv, 'w_proj': w_proj, 'b_proj': b_proj}
    _L0_attn_a_in = _L0_attn_a_setup()

    def _L0_attn_b_setup():
        import jax, jax.numpy as jnp
        import numpy as np
        EPS = float(np.finfo(np.float32).eps)
        SEQ_LEN = 512
        NUM_HEADS = 16
        DIM_EMB = 256
        DIM_HEAD = DIM_EMB // NUM_HEADS
        DIM_K = DIM_EMB
        BATCH = 2

        def cosine_positional_encoding(seq_len, dim):
            idx = jnp.arange(seq_len, dtype=jnp.float32)
            scale = 1.0 / (10000.0 ** (jnp.arange(0, dim, 2, dtype=jnp.float32) / dim) + EPS)
            ang = idx[:, None] * scale[None, :]
            return jnp.stack([jnp.sin(ang), jnp.cos(ang)], axis=-1).reshape(seq_len, dim)
        key = jax.random.key(seed)
        ks = jax.random.split(key, 5)
        s = DIM_EMB ** (-0.5)
        return {'x': jax.random.normal(ks[0], (BATCH, SEQ_LEN, DIM_EMB), dtype=jnp.float32), 'Wq': jax.random.normal(ks[1], (DIM_EMB, DIM_EMB), dtype=jnp.float32) * s, 'Wk': jax.random.normal(ks[2], (DIM_EMB, DIM_EMB), dtype=jnp.float32) * s, 'Wv': jax.random.normal(ks[3], (DIM_EMB, DIM_EMB), dtype=jnp.float32) * s, 'Wo': jax.random.normal(ks[4], (DIM_EMB, DIM_EMB), dtype=jnp.float32) * s}
    _L0_attn_b_in = _L0_attn_b_setup()

    def _L0_ffn_setup():
        import jax, jax.numpy as jnp
        import numpy as np
        B, S, K, N = (8, 2048, 256, 256)
        key = jax.random.key(seed)
        k1, k2, k3, k4 = jax.random.split(key, 4)
        x = jax.random.normal(k1, (B, S, K), dtype=jnp.float32)
        CB = jnp.clip(jnp.round(jax.random.normal(k2, (N, K), dtype=jnp.float32) * 42.0), -127.0, 127.0)
        SCB = jax.random.uniform(k3, (N,), dtype=jnp.float32, minval=0.5, maxval=2.0)
        bias = jax.random.normal(k4, (N,), dtype=jnp.float32) * 0.02
        return {'x': x, 'CB': CB, 'SCB': SCB, 'bias': bias}
    _L0_ffn_in = _L0_ffn_setup()
    _d = {'L0_attn_a_x': _L0_attn_a_in['x'], 'L0_attn_a_w_qkv': _L0_attn_a_in['w_qkv'], 'L0_attn_a_w_proj': _L0_attn_a_in['w_proj'], 'L0_attn_a_b_proj': _L0_attn_a_in['b_proj'], 'L0_attn_b_Wq': _L0_attn_b_in['Wq'], 'L0_attn_b_Wk': _L0_attn_b_in['Wk'], 'L0_attn_b_Wv': _L0_attn_b_in['Wv'], 'L0_attn_b_Wo': _L0_attn_b_in['Wo'], 'L0_ffn_CB': _L0_ffn_in['CB'], 'L0_ffn_SCB': _L0_ffn_in['SCB'], 'L0_ffn_bias': _L0_ffn_in['bias']}
    _x0 = _d['L0_attn_a_x']
    _d['L0_attn_a_x'] = jax.random.normal(jax.random.fold_in(jax.random.key(seed), 1), (4, 2048, 256), dtype=_x0.dtype)
    del _x0
    return _d

def reference(L0_attn_a_x, L0_attn_a_w_qkv, L0_attn_a_w_proj, L0_attn_a_b_proj, L0_attn_b_Wq, L0_attn_b_Wk, L0_attn_b_Wv, L0_attn_b_Wo, L0_ffn_CB, L0_ffn_SCB, L0_ffn_bias):

    def _L0_attn_a_ref(x, w_qkv, w_proj, b_proj):
        import jax, jax.numpy as jnp
        import numpy as np
        H = 16
        WIN = 64
        B, N, C = x.shape
        D = C // H
        scale = D ** (-0.5)
        b = WIN // 2
        nb = N // b
        qkv = (x @ w_qkv).reshape(B, N, 3, H, D).transpose(2, 0, 3, 1, 4)
        q, k, v = (qkv[0], qkv[1], qkv[2])
        qb = q.reshape(B, H, nb, b, D)
        kp = jnp.pad(k, ((0, 0), (0, 0), (b, b), (0, 0)))
        vp = jnp.pad(v, ((0, 0), (0, 0), (b, b), (0, 0)))
        win_idx = jnp.arange(nb)[:, None] * b + jnp.arange(3 * b)[None, :]
        kw = kp[:, :, win_idx]
        vw = vp[:, :, win_idx]
        scores = jnp.einsum('bhnqd,bhnkd->bhnqk', qb, kw) * scale
        qi = jnp.arange(b)[:, None]
        ki = jnp.arange(3 * b)[None, :]
        rel_ok = jnp.abs(ki - b - qi) <= b
        key_pos = jnp.arange(nb)[:, None] * b + jnp.arange(3 * b)[None, :] - b
        in_range = (key_pos >= 0) & (key_pos < N)
        valid = rel_ok[None, :, :] & in_range[:, None, :]
        scores = jnp.where(valid[None, None], scores, -jnp.inf)
        attn = jax.nn.softmax(scores, axis=-1)
        out = jnp.einsum('bhnqk,bhnkd->bhnqd', attn, vw)
        out = out.reshape(B, H, N, D).transpose(0, 2, 1, 3).reshape(B, N, C)
        return out @ w_proj + b_proj

    def _L0_attn_b_ref(x, Wq, Wk, Wv, Wo):
        import jax, jax.numpy as jnp
        import numpy as np
        EPS = float(np.finfo(np.float32).eps)
        SEQ_LEN = 512
        NUM_HEADS = 16
        DIM_EMB = 256
        DIM_HEAD = DIM_EMB // NUM_HEADS
        DIM_K = DIM_EMB
        BATCH = 2

        def cosine_positional_encoding(seq_len, dim):
            idx = jnp.arange(seq_len, dtype=jnp.float32)
            scale = 1.0 / (10000.0 ** (jnp.arange(0, dim, 2, dtype=jnp.float32) / dim) + EPS)
            ang = idx[:, None] * scale[None, :]
            return jnp.stack([jnp.sin(ang), jnp.cos(ang)], axis=-1).reshape(seq_len, dim)
        B, S, E = x.shape
        pos = cosine_positional_encoding(S, DIM_HEAD)

        def split_heads(t):
            return t.reshape(B, S, NUM_HEADS, DIM_HEAD).transpose(0, 2, 1, 3)
        q = split_heads(x @ Wq) + pos[None, None]
        k = split_heads(x @ Wk) + pos[None, None]
        v = split_heads(x @ Wv)
        scores = jnp.einsum('bhqd,bhkd->bhqk', q, k) * DIM_K ** (-0.5)
        causal_mask = jnp.triu(jnp.ones((S, S), dtype=bool), k=1)
        m_inf = -jnp.finfo(scores.dtype).max
        scores = jnp.where(causal_mask[None, None], m_inf, scores)
        attn = jax.nn.softmax(scores, axis=-1)
        out = jnp.einsum('bhqk,bhkd->bhqd', attn, v)
        out = out.transpose(0, 2, 1, 3).reshape(B, S, E)
        return out @ Wo

    def _L0_ffn_ref(x, CB, SCB, bias):
        import jax, jax.numpy as jnp
        import numpy as np
        B, S, K, N = (8, 2048, 256, 256)
        out = jnp.einsum('bsk,nk->bsn', x, CB)
        out = out * (SCB * (1.0 / 127.0)) + bias
        return out
    x = L0_attn_a_x
    x = x + _L0_attn_a_ref(_layernorm(x, axis=-1), L0_attn_a_w_qkv, L0_attn_a_w_proj, L0_attn_a_b_proj)
    x = x + _L0_ffn_ref(_layernorm(x, axis=-1), L0_ffn_CB, L0_ffn_SCB, L0_ffn_bias)
    x = x + _L0_attn_b_ref(_layernorm(x, axis=-1), L0_attn_b_Wq, L0_attn_b_Wk, L0_attn_b_Wv, L0_attn_b_Wo)
    x = x + _L0_ffn_ref(_layernorm(x, axis=-1), L0_ffn_CB, L0_ffn_SCB, L0_ffn_bias)
    return x

_drawn_inputs = setup_inputs


def setup_inputs(seed=0):
    import zlib

    import numpy as np

    out = dict(_drawn_inputs(seed))
    spreads = {}
    factors = {'L0_attn_a_w_qkv': 4.423,
     'L0_attn_a_w_proj': 4.395,
     'L0_attn_a_b_proj': 3.149,
     'L0_attn_b_Wq': 8.0,
     'L0_attn_b_Wk': 8.0,
     'L0_attn_b_Wv': 5.509,
     'L0_attn_b_Wo': 5.424,
     'L0_ffn_bias': 8.0}
    for name, (base, spread) in spreads.items():
        noise = np.random.default_rng([zlib.crc32(name.encode()), seed]).standard_normal(out[name].shape)
        drawn = base * np.exp(spread * noise) if base else spread * noise
        out[name] = jnp.asarray(drawn.astype(out[name].dtype))
    for name, factor in factors.items():
        out[name] = (out[name] * factor).astype(out[name].dtype)
    return out
```

```python
from contextlib import ExitStack, contextmanager

import numpy as np
import concourse.bass as bass
from concourse import mybir

F32 = mybir.dt.float32
BF16 = mybir.dt.bfloat16
ALU = mybir.AluOpType
ACT = mybir.ActivationFunctionType
AX = mybir.AxisListType.X

P = 128
B, S, C = 4, 2048, 256
H, D = 16, 16
HG = 4
NG = H // HG
STEPS = B * NG
KC = C // P
QG = 4
GW = S // QG
TG = GW // P
NT = S // P
WIN = 32
WQ = 64
NW = S // WQ
PAD = WIN
SP_ = S + 2 * PAD
PARTS = 3
ROWS = 6 * D
VW = D + 1
NEG = -1e30
LOWEST = -3e38
EPS = 1e-5
BUFS = 3
LOOPS = (STEPS - 1) // BUFS

Q_BLOCKS = [(0, 2, 0), (0, 2, 2), (2, 1, 4), (0, 1, 5)]
K_BLOCKS = [(0, 1, 0), (0, 1, 1), (1, 1, 2), (1, 1, 3), (0, 1, 4), (2, 1, 5)]
ROW_LOADS = len(Q_BLOCKS) + len(K_BLOCKS)


def constants():
    f = np.float32
    ident = np.eye(P, dtype=f)
    spread = np.zeros((P, P), f)
    for j in range(HG):
        spread[32 * j + D, 32 * j:32 * j + 32] = 1.0
    k, q = np.arange(P)[:, None], np.arange(P)[None, :]
    causal_kq = np.where(k > q, NEG, 0.0).astype(f)
    causal_q = np.zeros((P, GW), f)
    causal_q[:, GW - P:] = causal_kq.T
    kk = np.arange(P + 2 * WIN)[None, :]
    qq = np.arange(P)[:, None]
    mid = (kk - qq >= 0) & (kk - qq <= 2 * WIN)
    first, last = mid & (kk >= WIN), mid & (kk < P + WIN)
    win_q = np.stack([np.concatenate([first, mid], 1), np.concatenate([mid, mid], 1),
                      np.concatenate([mid, last], 1)], 1)
    win_q = np.where(win_q, 0.0, NEG).astype(f)
    qq = np.arange(WQ)[None, :]
    mid = (k - qq >= 0) & (k - qq <= 2 * WIN)
    first, last = mid & (k >= WIN), mid & (k < P - WIN)
    n = GW // WQ
    win_k = np.stack([np.concatenate([first] + [mid] * (n - 1), 1), np.concatenate([mid] * n, 1),
                      np.concatenate([mid] * (n - 1) + [last], 1)], 1)
    win_k = np.where(win_k, 0.0, NEG).astype(f)
    idx = np.arange(S, dtype=f)
    scale = (f(1.0) / (np.power(f(10000.0), np.arange(0, D, 2, dtype=f) / f(D)) + np.finfo(f).eps)).astype(f)
    ang = (idx[:, None] * scale[None, :]).astype(f)
    pos = np.stack([np.sin(ang), np.cos(ang)], -1).reshape(S, D).astype(f)
    pos_t = np.ascontiguousarray(np.tile(pos.T, (P // D, 1)))
    return {"ident": ident, "spread": spread, "causal_kq": causal_kq, "causal_q": causal_q,
            "win_q": np.ascontiguousarray(win_q.reshape(P, -1)), "win_k": np.ascontiguousarray(win_k.reshape(P, -1)),
            "pos_t": pos_t}


class Memory:

    def __init__(self, nc, ctx, first_sem, tag):
        self.nc, self.ctx, self.first_sem, self.tag, self.sems = nc, ctx, first_sem, tag, []

    def sb(self, name, shape, dt=F32):
        return self.ctx.enter_context(self.nc.sbuf_tensor(f"{self.tag}_{name}", shape, dt))

    def ps(self, name, shape):
        return self.ctx.enter_context(self.nc.psum_tensor(f"{self.tag}_{name}", shape, F32))

    def sem(self, name):
        s = self.ctx.enter_context(self.nc.semaphore(f"{self.tag}_{name}", num=self.first_sem + len(self.sems)))
        self.sems.append(s)
        return s

    def barrier_and_clear(self):
        nc = self.nc
        first = self.first_sem
        nc.multi_engine_barrier([nc.tensor.engine, nc.vector.engine, nc.scalar.engine, nc.gpsimd.engine,
                                 nc.sync.engine], sems_to_clear=range(first, first + len(self.sems)))


def setup_phase(nc, dram, con, w):
    with ExitStack() as ctx:
        m = Memory(nc, ctx, w["first_sem"], "setup")
        loaded, cb_scaled, cb_turned, done = (m.sem(n) for n in ("loaded", "cb_scaled", "cb_turned", "done"))
        cb = m.sb("cb", [P, KC, C])
        scb = m.sb("scb", [P, KC])
        turned = [m.ps(f"turned{k}", [P, 512]) for k in range(KC)]
        with nc.Block() as block:
            @block.sync
            def _(sp):
                def rows(x):
                    return x.rearrange("(k p) n -> p k n", p=P)
                loads = [(w["qkv_a"][:], rows(dram["w_qkv"])), (w["proj_a"][:], rows(dram["w_proj"])),
                         (w["qkv_b"][:, :, 0:C], rows(dram["Wq"])), (w["qkv_b"][:, :, C:2 * C], rows(dram["Wk"])),
                         (w["qkv_b"][:, :, 2 * C:3 * C], rows(dram["Wv"])), (w["proj_b"][:], rows(dram["Wo"])),
                         (cb[:], rows(dram["CB"])), (scb[:], dram["SCB"].rearrange("(k p) -> p k", p=P)),
                         (w["b_proj"][:], dram["b_proj"].rearrange("(o n) -> o n", o=1).broadcast_to([P, C])),
                         (w["b_ffn"][:], dram["b_ffn"].rearrange("(o n) -> o n", o=1).broadcast_to([P, C])),
                         (w["ident"][:], con["ident"])]
                for dst, src in loads:
                    sp.dma_start(dst, src, allow_slow_non_contiguous=True).then_inc(loaded, 16)
                sp.wait_ge(loaded, 16 * len(loads))

            @block.vector
            def _(dve):
                dve.wait_ge(loaded, 16 * 11)
                for k in range(KC):
                    dve.tensor_scalar(cb[:, k, :], cb[:, k, :], scb[:, k:k + 1], 1.0 / 127.0,
                                      ALU.mult, ALU.mult).then_inc(cb_scaled, 1)
                dve.tensor_copy(w["ident_b"][:], w["ident"][:]).then_inc(done, 1)
                for k in range(KC):
                    dve.wait_ge(cb_turned, k + 1)
                    dve.tensor_copy(w["ffn"][:, k, :], turned[k][:, 0:C]).then_inc(done, 1)

            @block.tensor
            def _(pe):
                pe.wait_ge(loaded, 16 * 11)
                pe.wait_ge(cb_scaled, KC)
                for k in range(KC):
                    for n in range(KC):
                        last = pe.transpose(turned[k][:, n * P:(n + 1) * P], cb[:, n, k * P:(k + 1) * P], w["ident"][:])
                    last.then_inc(cb_turned, 1)
        m.barrier_and_clear()


def token_phase(nc, dram, con, w, scr, tag, src, dst, attn_in, w_proj, b_proj, has_ffn, w_qkv, pos, windows):
    stages = (["project"] if w_proj is not None else []) + (["norm_f", "ffn"] if has_ffn else []) + (
        ["norm_q", "qkv"] if w_qkv is not None else [])
    with ExitStack() as ctx:
        m = Memory(nc, ctx, w["first_sem"], tag)
        X = m.sb("X", [P, NT, C])
        stats = m.sb("stats", [P, TG, 6])
        mv = m.sb("mv", [P, TG, 2])
        var = m.sb("var", [P, TG])
        rstd = m.sb("rstd", [P, TG])
        power = m.sb("power", [P, TG])
        xn = m.sb("xn", [P, 2, TG, C])
        t_bank = [m.ps(f"t_bank{k}", [P, GW]) for k in range(KC)]
        y_bank = [m.ps(f"y_bank{k}", [P, 2, C]) for k in range(2)]
        x_in = [m.sem(f"x_in{g}") for g in range(QG)]
        x_out = m.sem("x_out")
        consts_in, power_set = m.sem("consts_in"), m.sem("power_set")
        stats_done, mv_done, var_done, rstd_done = (m.sem(n) for n in ("stats_done", "mv_done", "var_done", "rstd_done"))
        xn_done, turned, turned_out = m.sem("xn_done"), m.sem("turned"), m.sem("turned_out")
        y_done, y_added, biased = m.sem("y_done"), m.sem("y_added"), m.sem("biased")
        if w_proj is not None:
            at = m.sb("at", [P, KC, S])
            at_in = [m.sem(f"at_in{g}") for g in range(QG)]
        if has_ffn:
            xT_f = m.sb("xT_f", [P, KC, GW])
        if w_qkv is not None:
            xT_q = m.sb("xT_q", [P, KC, SP_])
            F = m.sb("F", [P, 2, GW])
            R = m.sb("R", [P, 2, GW])
            parts = m.sb("parts", [P, 2, PARTS, GW], BF16)
            v_rows = m.sb("v_rows", [P, 2, 2, H, VW])
            qk_bank = [m.ps(f"qk_bank{k}", [P, GW]) for k in range(2)]
            v_bank = [m.ps(f"v_bank{k}", [P, 2, C]) for k in range(2)]
            qk_done, f_done, hi_done, rest_done, mid_done, low_done = (
                m.sem(n) for n in ("qk_done", "f_done", "hi_done", "rest_done", "mid_done", "low_done"))
            parts_out = [m.sem(f"parts_out{i}") for i in range(2)]
            v_done, v_copied = m.sem("v_done"), m.sem("v_copied")
            v_out = [m.sem(f"v_out{i}") for i in range(2)]
            if pos:
                pos_sb = m.sb("pos", [P, S])
            if windows:
                v_pairs = [[(WQ * u, u) for u in (2 * p, 2 * p + 1)] for p in range(NW // 2)]
                ready = lambda g: [p for p in range(NW // 2) if min(QG - 1, (WQ * (2 * p + 1) + P - PAD - 1) // GW) == g]
            else:
                v_pairs = [[(PAD + P * u, u) for u in (2 * p, 2 * p + 1)] for p in range(NT // 2)]
                ready = lambda g: [p for p in range(NT // 2) if p // (TG // 2) == g]

        with nc.Block() as block:
            @block.vector
            def _(dve):
                n = 1
                dve.memset(power[:], -0.5).then_inc(power_set, 1)
                if w_qkv is not None:
                    dve.memset(xT_q[:, :, 0:PAD], 0.0).then_inc(power_set, 1)
                    dve.memset(xT_q[:, :, PAD + S:SP_], 0.0).then_inc(power_set, 1)
                    dve.memset(v_rows[:], 1.0).then_inc(power_set, 1)
                    n += 3
                dve.wait_ge(power_set, n)
                if pos:
                    dve.wait_ge(consts_in, 16)

            @block.sync
            def _(sp):
                if pos:
                    sp.dma_start(pos_sb[:], con["pos_t"]).then_inc(consts_in, 16)
                    sp.wait_ge(consts_in, 16)
        m.barrier_and_clear()

        def slots():
            for t in range(QG + len(stages) - 1):
                for n in reversed(range(len(stages))):
                    if 0 <= t - n < QG:
                        yield stages[n], t - n

        norms = [s for s in stages if s.startswith("norm")]

        Y = {"project": 2, "ffn": 2}
        TURN = {"norm_f": KC, "norm_q": KC}

        def upto(per, stage, g):
            n = 0
            for s, gg in slots():
                n += per.get(s, 0)
                if (s, gg) == (stage, g):
                    return n

        def biased_by(stage, g):
            if stage == "project":
                return g + 1
            return (QG if b_proj is not None else 0) + upto({"norm_f": 1}, "norm_f", g)

        @contextmanager
        def batches():
            with nc.Fori(0, B) as b:
                with nc.Block() as block:
                    yield b, block
                m.barrier_and_clear()

        with batches() as (b, block):
            @block.sync
            def _(sp):
                x_src, x_dst = src(b), dst(b) if dst else None
                for g in range(QG):
                    sp.dma_start(X[:, g * TG:(g + 1) * TG, :], x_src[:, g * TG:(g + 1) * TG, :]).then_inc(x_in[g], 16)
                    if w_proj is not None:
                        sp.dma_start(at[:, :, g * GW:(g + 1) * GW],
                                     attn_in(b)[:, :, g * GW:(g + 1) * GW]).then_inc(at_in[g], 16)
                n_qk = n_v = n_y = n_out = 0
                last_add = "ffn" if has_ffn else "project"
                for stage, g in slots():
                    if stage in ("project", "ffn"):
                        n_y += 2
                    if dst and stage == last_add:
                        sp.wait_ge(y_added, n_y)
                        sp.dma_start(x_dst[:, g * TG:(g + 1) * TG, :], X[:, g * TG:(g + 1) * TG, :]).then_inc(x_out, 16)
                        n_out += 1
                    if stage == "qkv":
                        for which in range(2):
                            for oc in range(2):
                                sp.wait_ge(low_done, n_qk + 1)
                                sp.wait_ge(mid_done, n_qk + 1)
                                sp.wait_ge(hi_done, n_qk + 1)
                                for part in range(PARTS):
                                    sp.dma_start(
                                        scr["qk"][which][b * 2 + oc, :, part, :, g * GW:(g + 1) * GW],
                                        parts[:, n_qk % 2, part, :]).then_inc(parts_out[n_qk % 2], 16)
                                n_qk += 1
                        for p in ready(g):
                            sp.wait_ge(v_copied, n_v + 1)
                            for i, (_, u) in enumerate(v_pairs[p]):
                                sp.dma_start(scr["v"][b, :, :, u, :].rearrange("h p c -> p h c"),
                                             v_rows[:, n_v % 2, i].rearrange("p (g j) c -> p g (j c)", g=NG)
                                             ).then_inc(v_out[n_v % 2], 16)
                            n_v += 1
                if n_out:
                    sp.wait_ge(x_out, 16 * n_out)
                if n_qk:
                    for i in range(2):
                        sp.wait_ge(parts_out[i], 16 * PARTS * (n_qk // 2))
                        sp.wait_ge(v_out[i], 32 * (n_v // 2))

            @block.vector
            def _(dve):
                n_norm = n_y = n_qk = 0
                for stage, g in slots():
                    tiles = range(g * TG, (g + 1) * TG)
                    if stage in ("project", "ffn"):
                        if stage == "project" and b_proj is None:
                            dve.wait_ge(x_in[g], 16)
                        else:
                            dve.wait_ge(biased, biased_by(stage, g))
                        for i in range(2):
                            t = g * TG + 2 * i
                            dve.wait_ge(y_done, n_y + 1)
                            dve.tensor_tensor(X[:, t:t + 2, :], y_bank[n_y % 2][:], X[:, t:t + 2, :],
                                              ALU.add).then_inc(y_added, 1)
                            n_y += 1
                    if stage in norms:
                        if stage == stages[0]:
                            dve.wait_ge(x_in[g], 16)
                        else:
                            dve.wait_ge(y_added, upto(Y, {"norm_f": "project", "norm_q": "ffn"}[stage], g))
                        if n_norm:
                            dve.wait_ge(rstd_done, n_norm)
                        for i, t in enumerate(tiles):
                            dve.bn_stats(stats[:, i, :], X[:, t, :]).then_inc(stats_done, 1)
                        dve.wait_ge(stats_done, TG * (n_norm + 1))
                        for i in range(TG):
                            dve.bn_aggr(mv[:, i, :], stats[:, i, :]).then_inc(mv_done, 1)
                        dve.wait_ge(rstd_done, n_norm + 1)
                        dve.wait_ge(mv_done, TG * (n_norm + 1))
                        if n_norm >= 2:
                            dve.wait_ge(turned, KC * (n_norm - 1))
                        for i, t in enumerate(tiles):
                            dve.tensor_scalar(xn[:, n_norm % 2, i, :], X[:, t, :], mv[:, i, 0:1], rstd[:, i:i + 1],
                                              ALU.subtract, ALU.mult).then_inc(xn_done, 1)
                        n_norm += 1
                        dve.wait_ge(xn_done, TG * n_norm)
                    if stage == "qkv":
                        def full(n, i):
                            dve.wait_ge(qk_done, n + 1)
                            if n >= 2:
                                dve.wait_ge(hi_done, n - 1)
                                dve.wait_ge(rest_done, n - 1)
                            if pos:
                                dve.tensor_tensor(F[:, n % 2, :], qk_bank[n % 2][:], pos_sb[:, g * GW:(g + 1) * GW],
                                                  ALU.add).then_inc(f_done, 1)
                            else:
                                dve.tensor_copy(F[:, n % 2, :], qk_bank[n % 2][:]).then_inc(f_done, 1)

                        def rest(n):
                            dve.wait_ge(f_done, n + 1)
                            dve.wait_ge(hi_done, n + 1)
                            if n >= 2:
                                dve.wait_ge(mid_done, n - 1)
                                dve.wait_ge(low_done, n - 1)
                            dve.tensor_tensor(R[:, n % 2, :], F[:, n % 2, :], parts[:, n % 2, 0, :],
                                              ALU.subtract).then_inc(rest_done, 1)
                        for i in range(4):
                            full(n_qk + i, i)
                            if i >= 1:
                                rest(n_qk + i - 1)
                        rest(n_qk + 3)
                        n_qk += 4

            @block.gpsimd
            def _(pool):
                n_norm = 0
                if b_proj is not None:
                    for g in range(QG):
                        pool.wait_ge(x_in[g], 16)
                        for t in range(g * TG, (g + 1) * TG):
                            last = pool.tensor_tensor(X[:, t, :], X[:, t, :], w[b_proj][:], ALU.add)
                        last.then_inc(biased, 1)
                n_qk = 0
                for stage, g in slots():
                    if stage in norms:
                        pool.wait_ge(mv_done, TG * (n_norm + 1))
                        if n_norm:
                            pool.wait_ge(xn_done, TG * n_norm)
                        pool.tensor_scalar(var[:], mv[:, :, 1], EPS, None, ALU.add).then_inc(var_done, 1)
                        pool.wait_ge(var_done, n_norm + 1)
                        pool.tensor_tensor(rstd[:], var[:], power[:], ALU.pow).then_inc(rstd_done, 1)
                        n_norm += 1
                        if stage == "norm_f":
                            pool.wait_ge(xn_done, TG * n_norm)
                            for t in range(g * TG, (g + 1) * TG):
                                last = pool.tensor_tensor(X[:, t, :], X[:, t, :], w["b_ffn"][:], ALU.add)
                            last.then_inc(biased, 1)
                    if stage == "qkv":
                        for i in range(4):
                            pool.wait_ge(rest_done, n_qk + 1)
                            pool.wait_ge(mid_done, n_qk + 1)
                            if n_qk >= 2:
                                pool.wait_ge(parts_out[n_qk % 2], 16 * PARTS * (n_qk // 2))
                            pool.tensor_tensor(parts[:, n_qk % 2, 2, :], R[:, n_qk % 2, :], parts[:, n_qk % 2, 1, :],
                                               ALU.subtract).then_inc(low_done, 1)
                            n_qk += 1

            @block.scalar
            def _(act):
                n_turn = n_qk = n_v = 0
                for stage, g in slots():
                    if stage in norms:
                        for k in range(KC):
                            act.wait_ge(turned, n_turn + 1)
                            if stage == "norm_f":
                                if g >= 1:
                                    act.wait_ge(y_done, upto(Y, "ffn", g - 1))
                                out = xT_f[:, k, :]
                            else:
                                out = xT_q[:, k, PAD + g * GW:PAD + (g + 1) * GW]
                            act.activation(out, t_bank[k][:], ACT.Copy).then_inc(turned_out, 1)
                            n_turn += 1
                    if stage == "qkv":
                        def hi(n):
                            act.wait_ge(f_done, n + 1)
                            if n >= 2:
                                act.wait_ge(parts_out[n % 2], 16 * PARTS * (n // 2))
                            act.activation(parts[:, n % 2, 0, :], F[:, n % 2, :], ACT.Copy).then_inc(hi_done, 1)

                        def mid(n):
                            act.wait_ge(rest_done, n + 1)
                            act.activation(parts[:, n % 2, 1, :], R[:, n % 2, :], ACT.Copy).then_inc(mid_done, 1)

                        def values(p):
                            nonlocal n_v
                            act.wait_ge(v_done, n_v + 1)
                            if n_v >= 2:
                                act.wait_ge(v_out[n_v % 2], 32 * (n_v // 2))
                            act.activation(v_rows[:, n_v % 2, :, :, 0:D],
                                           v_bank[n_v % 2][:].rearrange("p u (h d) -> p u h d", h=H),
                                           ACT.Copy).then_inc(v_copied, 1)
                            n_v += 1
                        todo = list(ready(g))
                        for i in range(4):
                            hi(n_qk + i)
                            if i >= 1:
                                mid(n_qk + i - 1)
                            elif todo:
                                values(todo.pop(0))
                        mid(n_qk + 3)
                        n_qk += 4
                        for p in todo:
                            values(p)

            @block.tensor
            def _(pe):
                n_norm = n_turn = n_y = n_qk = n_v = 0

                def rows_product(n, lhs, weights):
                    for i in range(2):
                        for k in range(KC):
                            last = pe.matmul(y_bank[n % 2][:, i, :], lhs(i, k), weights[:, k, :],
                                             start=(k == 0), stop=(k == KC - 1))
                    last.then_inc(y_done, 1)

                for stage, g in slots():
                    if stage == "project":
                        pe.wait_ge(at_in[g], 16)
                        for i in range(2):
                            if n_y >= 2:
                                pe.wait_ge(y_added, n_y - 1)
                            c0 = g * GW + 2 * i * P
                            rows_product(n_y, lambda t, k: at[:, k, c0 + t * P:c0 + (t + 1) * P], w[w_proj])
                            n_y += 1
                    if stage == "ffn":
                        pe.wait_ge(turned_out, upto(TURN, "norm_f", g))
                        for i in range(2):
                            if n_y >= 2:
                                pe.wait_ge(y_added, n_y - 1)
                            c0 = 2 * i * P
                            rows_product(n_y, lambda t, k: xT_f[:, k, c0 + t * P:c0 + (t + 1) * P], w["ffn"])
                            n_y += 1
                    if stage in norms:
                        pe.wait_ge(xn_done, TG * (n_norm + 1))
                        for k in range(KC):
                            if n_norm:
                                pe.wait_ge(turned_out, n_turn - KC + 1)
                            for i in range(TG):
                                last = pe.transpose(t_bank[k][:, i * P:(i + 1) * P],
                                                    xn[:, n_norm % 2, i, k * P:(k + 1) * P], w["ident"][:])
                            last.then_inc(turned, 1)
                            n_turn += 1
                        n_norm += 1
                    if stage == "qkv":
                        pe.wait_ge(turned_out, upto(TURN, "norm_q", g))

                        def values(p):
                            nonlocal n_v
                            if n_v >= 2:
                                pe.wait_ge(v_copied, n_v - 1)
                            for i, (c0, _) in enumerate(v_pairs[p]):
                                for k in range(KC):
                                    last = pe.matmul(v_bank[n_v % 2][:, i, :], xT_q[:, k, c0:c0 + P],
                                                     w[w_qkv][:, k, 2 * C:3 * C], start=(k == 0), stop=(k == KC - 1))
                            last.then_inc(v_done, 1)
                            n_v += 1
                        todo = list(ready(g))
                        for i in range(4):
                            if n_qk >= 2:
                                pe.wait_ge(f_done, n_qk - 1)
                            for k in range(KC):
                                last = pe.matmul(qk_bank[n_qk % 2][:], w[w_qkv][:, k, i * P:(i + 1) * P],
                                                 xT_q[:, k, PAD + g * GW:PAD + (g + 1) * GW],
                                                 start=(k == 0), stop=(k == KC - 1))
                            last.then_inc(qk_done, 1)
                            n_qk += 1
                            if i == 0 and todo:
                                values(todo.pop(0))
                        for p in todo:
                            values(p)



def attention_phase(nc, con, w, scr, tag, windows, score_scale):
    KW = P + 2 * WIN
    QT = NT
    if windows:
        units = [(g, None, None, 0) for g in range(QG)]
    else:
        units = [(g, kb, kb, max(0, kb - TG * g) * P) for g in range(QG) for kb in range(TG * (g + 1))]
    U = len(units)
    last_unit = {g: max(u for u in range(U) if units[u][0] == g) for g in range(QG)}
    if windows:
        jobs = [(g, j, t, 0, 2 * KW) for g in range(QG) for t in range(g * TG, (g + 1) * TG, 2) for j in range(HG)]
    else:
        jobs = [(t // TG, j, t, c, min(GW, (t + 1) * P - c * GW))
                for t in range(QT) for j in range(HG) for c in range(t // TG + 1)]
    weight = [sum(GW - x[3] for x in units[:u + 1]) for u in range(U)]
    cols = [sum(x[4] for x in jobs[:i + 1]) for i in range(len(jobs))]
    unit_of = [min(u for u in range(U) if cols[i] * weight[-1] <= weight[u] * cols[-1] + 1) for i in range(len(jobs))]
    jobs_at = [[i for i in range(len(jobs)) if unit_of[i] == u] for u in range(U)]
    group_jobs = [sum(1 for x in jobs if x[0] <= g) for g in range(QG)]
    max_end = [unit_of[group_jobs[g] - 1] for g in range(QG)]

    with ExitStack() as ctx:
        m = Memory(nc, ctx, w["first_sem"], tag)
        QA = m.sb("QA", [P, BUFS, HG, SP_], BF16)
        KA = m.sb("KA", [P, BUFS, HG, SP_], BF16)
        VT = NW if windows else NT
        V = m.sb("V", [P, BUFS, VT, HG, VW])
        probs = m.sb("probs", [P, 2, HG, GW])
        o_sb = m.sb("o_sb", [P, 2, GW])
        inv = m.sb("inv", [P, GW])
        o_norm = m.sb("o_norm", [P, 2, GW])
        part = m.sb("part", [P, HG, QT, QG])
        top = m.sb("top", [P, QG, HG, TG])
        low = m.sb("low", [HG * TG, P])
        rest = m.sb("rest", [HG * TG, P])
        low_parts = m.sb("low_parts", [HG * TG, 2, PARTS, P], BF16)
        spread = m.sb("spread", [P, P])
        if windows:
            mask_f = m.sb("mask_f", [P, 3 * GW])
            mask_k = m.sb("mask_k", [P, 3, GW], BF16)
            mask_q = m.sb("mask_q", [P, 3, 2 * KW], BF16)
        else:
            mask_f = m.sb("mask_f", [P, P])
            mask_k = m.sb("mask_k", [P, P], BF16)
            mask_q = m.sb("mask_q", [P, GW])
            junk = m.sb("junk", [P, 2, GW], BF16)
        s_bank = m.ps("s_bank", [P, 2, 2, GW])
        m_bank = [m.ps(f"m_bank{i}", [P, GW]) for i in range(2)]
        o_bank = m.ps("o_bank", [P, GW])
        x_bank = m.ps("x_bank", [P, GW])

        setup, set_in = m.sem("setup"), m.sem("set_in")
        qk_in = [m.sem(f"qk_in{k}") for k in range(BUFS)]
        v_in = [m.sem(f"v_in{k}") for k in range(BUFS)]
        low_kept = m.sem("low_kept")
        low_in = [[m.sem(f"low_in{k}{g}") for g in range(QG)] for k in range(BUFS)]
        out_done = [m.sem(f"out_done{i}") for i in range(2)]
        s_done, exp_done, pv_done = m.sem("s_done"), m.sem("exp_done"), m.sem("pv_done")
        m_done, m_free, part_done, top_done = m.sem("m_done"), m.sem("m_free"), m.sem("part_done"), m.sem("top_done")
        top_turned, low_done, split_1, split_2, split_3, split_4 = (
            m.sem(n) for n in ("top_turned", "low_done", "split_1", "split_2", "split_3", "split_4"))
        o_copied, sum_spread, inv_done, norm_done = (m.sem(n) for n in ("o_copied", "sum_spread", "inv_done", "norm_done"))

        def load(sp, step, buf, arrived):
            for blocks, dst, which in ((Q_BLOCKS, QA, 0), (K_BLOCKS, KA, 1)):
                for first, n, row in blocks:
                    src = scr["qk"][which].rearrange("o h p d s -> (o h) (p d) s")
                    src = src[bass.ds(step * HG, HG), first * D:(first + n) * D, :]
                    sp.dma_start(dst[row * D:(row + n) * D, buf, :, PAD:PAD + S],
                                 src.rearrange("j r s -> r j s")).then_inc(arrived, 16)

        def load_v(sp, step, buf, arrived):
            src = scr["v"].rearrange("b g p u c -> (b g) p u c")[bass.ds(step, 1)]
            sp.dma_start(V[:, buf].rearrange("p u j c -> p (u j c)"),
                         src.rearrange("o p u c -> (o p) (u c)")).then_inc(arrived, 16)

        with nc.Block() as block:
            @block.sync
            def _(sp):
                sp.dma_start(spread[:], con["spread"]).then_inc(set_in, 16)
                if windows:
                    sp.dma_start(mask_f[:, 0:3 * GW], con["win_k"]).then_inc(set_in, 16)
                    sp.wait_ge(setup, 1)
                    sp.dma_start(mask_f[:, 0:6 * KW], con["win_q"]).then_inc(set_in, 16)
                    sp.wait_ge(set_in, 48)
                else:
                    sp.dma_start(mask_f[:], con["causal_kq"]).then_inc(set_in, 16)
                    sp.dma_start(mask_q[:], con["causal_q"]).then_inc(set_in, 16)
                    sp.wait_ge(set_in, 48)

            @block.vector
            def _(dve):
                if windows:
                    dve.wait_ge(set_in, 32)
                    dve.tensor_copy(mask_k[:].rearrange("p a n -> p (a n)"), mask_f[:]).then_inc(setup, 1)
                    dve.wait_ge(set_in, 48)
                    dve.tensor_copy(mask_q[:].rearrange("p a n -> p (a n)"), mask_f[:, 0:6 * KW]).then_inc(setup, 1)
                else:
                    dve.wait_ge(set_in, 48)
                    dve.tensor_copy(mask_k[:], mask_f[:]).then_inc(setup, 1)
                    dve.memset(junk[:], 0.0).then_inc(setup, 1)
                dve.memset(part[:], LOWEST).then_inc(setup, 1)
                dve.memset(o_bank[:], 0.0).then_inc(setup, 1)
                dve.wait_ge(setup, 4)

            @block.gpsimd
            def _(pool):
                for X in (QA, KA):
                    pool.memset(X[:, :, :, 0:PAD], 0.0).then_inc(low_done, 1)
                    pool.memset(X[:, :, :, PAD + S:SP_], 0.0).then_inc(low_done, 1)
                pool.wait_ge(low_done, 4)
                pool.memset(KA[ROWS:ROWS + PARTS], 1.0).then_inc(low_done, 1)
                pool.wait_ge(low_done, 5)
        m.barrier_and_clear()

        def part_of_program(steps, loads, block, exp=True, first_max=0):
            K = len(steps)
            has_max = [not (exp and k == K - 1 and first_max < 0) for k in range(K)]
            NU = U if exp else U
            exp_buf = [k % BUFS for k in range(K)]
            max_buf = [(k + (1 if exp else 0)) % BUFS for k in range(K)]

            def x_uses(k):
                uses = []
                for u in range(U + 2):
                    for g in range(QG):
                        if exp and last_unit[g] + 2 == u:
                            uses.append((u, "sum", g))
                        if has_max[k] and max_end[g] + 1 == u:
                            uses.append((u, "top", g))
                return uses
            uses = [(k, *x) for k in range(K) for x in x_uses(k)]

            def uses_before(k, u, kind, g):
                i = uses.index((k, u, kind, g))
                return (sum(1 for x in uses[:i] if x[2] == "sum"), sum(1 for x in uses[:i] if x[2] == "top"),
                        uses[i - 1][2] if i else None)

            @block.sync
            def _(sp):
                n_low = n_out = 0
                for k in range(K):
                    if loads[k] is not None:
                        if exp and k:
                            sp.wait_ge(pv_done, k * U)
                        (qk_step, qk_buf), (v_step, v_buf) = loads[k]
                        load(sp, qk_step, qk_buf, qk_in[k])
                        load_v(sp, v_step, v_buf, v_in[k])
                    for u in range(U + 2):
                        for g in range(QG):
                            if has_max[k] and max_end[g] + 1 == u:
                                sp.wait_ge(split_4, n_low + 1)
                                kept = scr["low"][n_low % (BUFS * QG)]
                                sp.dma_start(kept.rearrange("r j (t q) -> (j t) r q", t=TG),
                                             low_parts[:, n_low % 2]).then_inc(low_kept, 16)
                                sp.wait_ge(low_kept, 16 * (n_low + 1))
                                sp.dma_start(QA[ROWS:ROWS + PARTS, max_buf[k], :, PAD + g * GW:PAD + (g + 1) * GW],
                                             kept).then_inc(low_in[k][g], 16)
                                n_low += 1
                            if exp and last_unit[g] + 2 == u:
                                sp.wait_ge(norm_done, n_out + 1)
                                for j in range(HG):
                                    dst = scr["attn"].rearrange("b (g j d) s -> (b g) j d s", g=NG, j=HG)
                                    dst = dst[bass.ds(steps[k], 1), j, :, g * GW:(g + 1) * GW]
                                    sp.dma_start(dst.rearrange("o d s -> (o d) s"),
                                                 o_norm[32 * j:32 * j + D, n_out % 2, :]).then_inc(out_done[n_out % 2], 16)
                                n_out += 1
                for k in range(K):
                    if loads[k] is not None:
                        sp.wait_ge(qk_in[k], 16 * ROW_LOADS)
                        sp.wait_ge(v_in[k], 16)
                    if has_max[k]:
                        for g in range(QG):
                            sp.wait_ge(low_in[k][g], 16)
                if exp:
                    for i in range(2):
                        sp.wait_ge(out_done[i], 16 * HG * (n_out // 2))

            @block.tensor
            def _(pe):
                n_job = n_half = n_pv = 0

                def scores(k, u):
                    nonlocal n_half
                    g, kb, _, off = units[u]
                    buf = exp_buf[k]
                    if k and u == last_unit.get(g - 1, -1) + 1:
                        pe.wait_ge(low_in[k - 1][g], 16)
                    for half in range(2):
                        if n_half >= 2:
                            pe.wait_ge(exp_done, n_half - 1)
                        for i in range(2):
                            j = 2 * half + i
                            bank = s_bank[:, n_half % 2, i, :]
                            if windows:
                                v = 0 if g == 0 else 2 if g == QG - 1 else 1
                                pe.matmul(bank, w["ident_b"][:], mask_k[:, v, :], start=True, stop=False)
                                for n in range(GW // WQ):
                                    q0 = g * GW + n * WQ
                                    last = pe.matmul(bank[:, n * WQ:(n + 1) * WQ], KA[0:ROWS + PARTS, buf, j, q0:q0 + P],
                                                     QA[0:ROWS + PARTS, buf, j, PAD + q0:PAD + q0 + WQ],
                                                     start=False, stop=(n == GW // WQ - 1))
                            else:
                                diag = kb >= TG * g
                                last = pe.matmul(bank[:, off:GW], KA[0:ROWS + PARTS, buf, j, PAD + kb * P:PAD + (kb + 1) * P],
                                                 QA[0:ROWS + PARTS, buf, j, PAD + g * GW + off:PAD + (g + 1) * GW],
                                                 start=True, stop=not diag)
                                if diag:
                                    last = pe.matmul(bank[:, off:off + P], w["ident_b"][:], mask_k[:],
                                                     start=False, stop=True)
                        last.then_inc(s_done, 1)
                        n_half += 1

                def values(k, u):
                    nonlocal n_pv
                    g, kb, _, off = units[u]
                    buf = exp_buf[k]
                    pe.wait_ge(exp_done, 2 * n_pv + 2)
                    if u == 0 and k:
                        pe.wait_ge(v_in[k - 1], 16)
                    first = u == last_unit.get(g - 1, -1) + 1
                    if first and k * QG + g:
                        pe.wait_ge(o_copied, k * QG + g)
                    if windows:
                        for n in range(GW // WQ):
                            for j in range(HG):
                                last = pe.matmul(o_bank[32 * j:32 * j + VW, n * WQ:(n + 1) * WQ],
                                                 V[:, buf, g * (GW // WQ) + n, j, :],
                                                 probs[:, n_pv % 2, j, n * WQ:(n + 1) * WQ], start=True, stop=True)
                    else:
                        for j in range(HG):
                            last = pe.matmul(o_bank[32 * j:32 * j + VW, off:GW], V[:, buf, kb, j, :],
                                             probs[:, n_pv % 2, j, off:GW], start=first, stop=(u == last_unit[g]))
                    last.then_inc(pv_done, 1)
                    n_pv += 1

                def maxima(k, i):
                    nonlocal n_job
                    g, j, t, c, n = jobs[i]
                    buf = max_buf[k]
                    if n_job >= 2:
                        pe.wait_ge(m_free, n_job - 1)
                    bank = m_bank[n_job % 2]
                    q_tile = lambda t: QA[0:ROWS, buf, j, PAD + t * P:PAD + (t + 1) * P]
                    if windows:
                        v = 0 if t == 0 else 2 if t == QT - 2 else 1
                        pe.matmul(bank[:, 0:n], w["ident_b"][:], mask_q[:, v, :], start=True, stop=False)
                        for x in range(2):
                            last = pe.matmul(bank[:, x * KW:(x + 1) * KW], q_tile(t + x),
                                             KA[0:ROWS, buf, j, (t + x) * P:(t + x) * P + KW], start=False, stop=(x == 1))
                    else:
                        last = pe.matmul(bank[:, 0:n], q_tile(t), KA[0:ROWS, buf, j, PAD + c * GW:PAD + c * GW + n],
                                         start=True, stop=True)
                    last.then_inc(m_done, 1)
                    n_job += 1

                def take_x_bank(k, u, kind, g):
                    sums, tops, before = uses_before(k, u, kind, g)
                    if before == "sum":
                        pe.wait_ge(inv_done, sums)
                    if before == "top":
                        pe.wait_ge(low_done, tops)

                for k in range(K):
                    if has_max[k] and exp and k:
                        pe.wait_ge(qk_in[k - 1], 16 * ROW_LOADS)
                    for u in range(U + 2):
                        if exp and u < U:
                            scores(k, u)
                        if has_max[k] and u < U:
                            for i in jobs_at[u]:
                                maxima(k, i)
                        if exp and 1 <= u <= U:
                            values(k, u - 1)
                        for g in range(QG):
                            if exp and last_unit[g] + 2 == u:
                                take_x_bank(k, u, "sum", g)
                                pe.wait_ge(o_copied, k * QG + g + 1)
                                pe.matmul(x_bank[:], spread[:], o_sb[:, (k * QG + g) % 2, :], start=True,
                                          stop=True).then_inc(sum_spread, 1)
                            if has_max[k] and max_end[g] + 1 == u:
                                take_x_bank(k, u, "top", g)
                                pe.wait_ge(top_done, k * QG + g + 1)
                                pe.transpose(x_bank[0:HG * TG, 0:P], top[:, g].rearrange("p j t -> p (j t)"),
                                             w["ident"][:]).then_inc(top_turned, 1)

            @block.scalar
            def _(act):
                n_half = n_pv = 0
                for k in range(K):
                    for u in range(U + 2):
                        if exp and u < U:
                            off = units[u][3]
                            for half in range(2):
                                act.wait_ge(s_done, n_half + 1)
                                if n_pv >= 2 and half == 0:
                                    act.wait_ge(pv_done, n_pv - 1)
                                act.activation(probs[:, n_pv % 2, 2 * half:2 * half + 2, off:GW],
                                               s_bank[:, n_half % 2, :, off:GW], ACT.Exp,
                                               scale=score_scale).then_inc(exp_done, 1)
                                n_half += 1
                            n_pv += 1
                        for g in range(QG):
                            if exp and last_unit[g] + 1 == u:
                                n = k * QG + g
                                act.wait_ge(pv_done, k * U + last_unit[g] + 1)
                                if n >= 2:
                                    act.wait_ge(sum_spread, n - 1)
                                    act.wait_ge(norm_done, n - 1)
                                act.activation(o_sb[:, n % 2, :], o_bank[:], ACT.Copy).then_inc(o_copied, 1)
                            if has_max[k] and max_end[g] + 1 == u:
                                n = k * QG + g
                                act.wait_ge(top_turned, n + 1)
                                if n >= 1:
                                    act.wait_ge(split_2, n)
                                act.activation(low[:], x_bank[0:HG * TG, 0:P], ACT.Copy, scale=-1.0).then_inc(low_done, 1)

            @block.vector
            def _(dve):
                n_job = 0
                for k in range(K):
                    for u in range(U + 3):
                        if has_max[k] and u < U:
                            for i in jobs_at[u]:
                                g, j, t, c, n = jobs[i]
                                bank = m_bank[n_job % 2]
                                dve.wait_ge(m_done, n_job + 1)
                                if windows:
                                    ins = dve.tensor_reduce(part[:, j, t:t + 2, 0], bank[:, 0:2 * KW].rearrange(
                                        "p (x n) -> p x n", x=2), AX, ALU.max)
                                elif c == t // TG:
                                    if n_job >= 2:
                                        dve.wait_ge(m_free, n_job - 1)
                                    ins = dve.tensor_tensor_reduce(junk[:, n_job % 2, 0:n], bank[:, 0:n], mask_q[:, GW - n:GW], 1.0,
                                                                   LOWEST, ALU.add, ALU.max, part[:, j, t, c:c + 1])
                                else:
                                    ins = dve.tensor_reduce(part[:, j, t, c:c + 1], bank[:, 0:n], AX, ALU.max)
                                ins.then_inc(m_free, 1)
                                n_job += 1
                                if group_jobs[g] == i + 1:
                                    dve.wait_ge(m_free, n_job)
                                    if k:
                                        dve.wait_ge(top_turned, (k - 1) * QG + g + 1)
                                    dve.tensor_reduce(top[:, g], part[:, :, g * TG:(g + 1) * TG, :], AX,
                                                      ALU.max).then_inc(top_done, 1)
                        for g in range(QG):
                            if exp and last_unit[g] + 2 == u:
                                n = k * QG + g
                                dve.wait_ge(sum_spread, n + 1)
                                if n >= 1:
                                    dve.wait_ge(norm_done, n)
                                dve.reciprocal(inv[:], x_bank[:]).then_inc(inv_done, 1)

            @block.gpsimd
            def _(pool):
                for k in range(K):
                    for u in range(U + 2):
                        for g in range(QG):
                            n = k * QG + g
                            if has_max[k] and max_end[g] + 1 == u:
                                half = low_parts[:, n % 2]
                                pool.wait_ge(low_done, n + 1)
                                if n >= 2:
                                    pool.wait_ge(low_kept, 16 * (n - 1))
                                pool.tensor_copy(half[:, 0, :], low[:]).then_inc(split_1, 1)
                                pool.wait_ge(split_1, n + 1)
                                pool.tensor_tensor(rest[:], low[:], half[:, 0, :], ALU.subtract).then_inc(split_2, 1)
                                pool.wait_ge(split_2, n + 1)
                                pool.tensor_copy(half[:, 1, :], rest[:]).then_inc(split_3, 1)
                                pool.wait_ge(split_3, n + 1)
                                pool.tensor_tensor(half[:, 2, :], rest[:], half[:, 1, :],
                                                   ALU.subtract).then_inc(split_4, 1)
                            if exp and last_unit[g] + 2 == u:
                                pool.wait_ge(inv_done, n + 1)
                                pool.wait_ge(o_copied, n + 1)
                                if n >= 2:
                                    pool.wait_ge(out_done[n % 2], 16 * HG * (n // 2))
                                pool.tensor_tensor(o_norm[:, n % 2, :], o_sb[:, n % 2, :], inv[:],
                                                   ALU.mult).then_inc(norm_done, 1)

        with nc.Block() as block:
            @block.sync
            def _(sp):
                for n in range(2):
                    load(sp, n, n, qk_in[n])
                load_v(sp, 0, 0, v_in[0])
                for n in range(2):
                    sp.wait_ge(qk_in[n], 16 * ROW_LOADS)
                sp.wait_ge(v_in[0], 16)
        m.barrier_and_clear()
        with nc.Block() as block:
            part_of_program([0], [None], block, exp=False)
        m.barrier_and_clear()
        with nc.Fori(0, LOOPS) as i:
            with nc.Block() as block:
                part_of_program([BUFS * i + k for k in range(BUFS)],
                                [(((BUFS * i + k + 2) % STEPS, (k + 2) % BUFS), (BUFS * i + k + 1, (k + 1) % BUFS))
                                 for k in range(BUFS)], block)
            m.barrier_and_clear()
        with nc.Block() as block:
            part_of_program([STEPS - 1], [None], block, first_max=-1)
        m.barrier_and_clear()


def program(nc, dram, con, out):
    with ExitStack() as ctx:
        def sb(name, shape, dt=F32):
            return ctx.enter_context(nc.sbuf_tensor(name, shape, dt))
        with nc.semaphore("lowest_free") as lowest:
            first_sem = lowest.num
        w = {"first_sem": first_sem, "qkv_a": sb("qkv_a", [P, KC, 3 * C]), "qkv_b": sb("qkv_b", [P, KC, 3 * C]),
             "proj_a": sb("proj_a", [P, KC, C]), "proj_b": sb("proj_b", [P, KC, C]), "ffn": sb("ffn", [P, KC, C]),
             "b_proj": sb("b_proj", [P, C]), "b_ffn": sb("b_ffn", [P, C]),
             "ident": sb("ident", [P, P]), "ident_b": sb("ident_b", [P, P], BF16)}
        x2 = nc.dram_tensor("x2", (B, S, C), F32, kind="Internal").ap()
        qk = [nc.dram_tensor(n, (B * 2, H // 2, PARTS, D, S), BF16, kind="Internal").ap() for n in ("q_parts", "k_parts")]
        v_w = nc.dram_tensor("v_w", (B, NG, P, NW, HG * VW), F32, kind="Internal").ap()
        v_t = nc.dram_tensor("v_t", (B, NG, P, NT, HG * VW), F32, kind="Internal").ap()
        low = nc.dram_tensor("low_maxima", (BUFS * QG, PARTS, HG, GW), BF16, kind="Internal").ap()
        attn = nc.dram_tensor("attn", (B, C, S), F32, kind="Internal").ap()

        def rows(x):
            return lambda b: x[bass.ds(b, 1)].rearrange("o (t p) c -> p (o t) c", p=P)

        def attn_in(b):
            return attn[bass.ds(b, 1)].rearrange("o (k p) s -> p (o k) s", p=P)
        setup_phase(nc, dram, con, w)
        token_phase(nc, dram, con, w, {"qk": qk, "v": v_w}, "first", rows(dram["x"]), None, None, None, None, False,
                    "qkv_a", False, True)
        attention_phase(nc, con, w, {"qk": qk, "v": v_w, "attn": attn, "low": low}, "window", True, D ** -0.5)
        token_phase(nc, dram, con, w, {"qk": qk, "v": v_t}, "middle", rows(dram["x"]), rows(x2), attn_in, "proj_a", "b_proj",
                    True, "qkv_b", True, False)
        attention_phase(nc, con, w, {"qk": qk, "v": v_t, "attn": attn, "low": low}, "causal", False, C ** -0.5)
        token_phase(nc, dram, con, w, None, "last", rows(x2), rows(out), attn_in, "proj_b", None, True, None, False, False)


_INS = {"x": "L0_attn_a_x", "w_qkv": "L0_attn_a_w_qkv", "w_proj": "L0_attn_a_w_proj", "b_proj": "L0_attn_a_b_proj",
        "Wq": "L0_attn_b_Wq", "Wk": "L0_attn_b_Wk", "Wv": "L0_attn_b_Wv", "Wo": "L0_attn_b_Wo",
        "CB": "L0_ffn_CB", "SCB": "L0_ffn_SCB", "b_ffn": "L0_ffn_bias"}


def kernel(**inputs):
    import numpy as _np
    import concourse.bacc as _bacc
    from concourse import mybir as _mybir
    from concourse.bass_utils import run_bass_kernel_spmd as _run

    nc = _bacc.Bacc("TRN2", target_bir_lowering=False, num_devices=1)
    arrays, dram, con = {}, {}, {}
    for short, name in _INS.items():
        a = _np.ascontiguousarray(inputs[name])
        arrays[f"in_{short}"] = a
        dram[short] = nc.dram_tensor(f"in_{short}", a.shape, _mybir.dt.from_np(a.dtype), kind="ExternalInput").ap()
    for name, a in constants().items():
        arrays[f"const_{name}"] = a
        con[name] = nc.dram_tensor(f"const_{name}", a.shape, _mybir.dt.from_np(a.dtype), kind="ExternalInput").ap()
    out = nc.dram_tensor("out_dram", (B, S, C), F32, kind="ExternalOutput").ap()
    program(nc, dram, con, out)
    r = _run(nc, [arrays], core_ids=[0])
    return r.results[0]["out_dram"]
```

```python
from contextlib import ExitStack, contextmanager

import numpy as np
import concourse.bass as bass
from concourse import mybir

F32 = mybir.dt.float32
BF16 = mybir.dt.bfloat16
ALU = mybir.AluOpType
ACT = mybir.ActivationFunctionType
AX = mybir.AxisListType.X

P = 128
B, S, C = 4, 2048, 256
H, D = 16, 16
HG = 4
NG = H // HG
STEPS = B * NG
KC = C // P
QG = 4
GW = S // QG
TG = GW // P
NT = S // P
WIN = 32
WQ = 64
NW = S // WQ
PAD = WIN
SP_ = S + 2 * PAD
RING = 4
PARTS = 3
ROWS = 6 * D
VW = D + 1
NEG = -1e30
LOWEST = -3e38
EPS = 1e-5
BUFS = 3
LOOPS = (STEPS - 1) // BUFS

Q_BLOCKS = [(0, 2, 0), (0, 2, 2), (2, 1, 4), (0, 1, 5)]
K_BLOCKS = [(0, 1, 0), (0, 1, 1), (1, 1, 2), (1, 1, 3), (0, 1, 4), (2, 1, 5)]
ROW_LOADS = len(Q_BLOCKS) + len(K_BLOCKS)


def constants():
    f = np.float32
    ident = np.eye(P, dtype=f)
    k, q = np.arange(P)[:, None], np.arange(P)[None, :]
    causal_kq = np.where(k > q, NEG, 0.0).astype(f)
    causal_q = np.zeros((P, GW), f)
    causal_q[:, GW - P:] = causal_kq.T
    kk = np.arange(P + 2 * WIN)[None, :]
    qq = np.arange(P)[:, None]
    mid = (kk - qq >= 0) & (kk - qq <= 2 * WIN)
    first, last = mid & (kk >= WIN), mid & (kk < P + WIN)
    win_q = np.stack([np.concatenate([first, mid], 1), np.concatenate([mid, mid], 1),
                      np.concatenate([mid, last], 1)], 1)
    win_q = np.where(win_q, 0.0, NEG).astype(f)
    qq = np.arange(WQ)[None, :]
    mid = (k - qq >= 0) & (k - qq <= 2 * WIN)
    first, last = mid & (k >= WIN), mid & (k < P - WIN)
    n = GW // WQ
    win_k = np.stack([np.concatenate([first] + [mid] * (n - 1), 1), np.concatenate([mid] * n, 1),
                      np.concatenate([mid] * (n - 1) + [last], 1)], 1)
    win_k = np.where(win_k, 0.0, NEG).astype(f)
    idx = np.arange(S, dtype=f)
    scale = (f(1.0) / (np.power(f(10000.0), np.arange(0, D, 2, dtype=f) / f(D)) + np.finfo(f).eps)).astype(f)
    ang = (idx[:, None] * scale[None, :]).astype(f)
    pos = np.stack([np.sin(ang), np.cos(ang)], -1).reshape(S, D).astype(f)
    pos_t = np.ascontiguousarray(np.tile(pos.T, (P // D, 1)))
    return {"ident": ident, "causal_kq": causal_kq, "causal_q": causal_q,
            "win_q": np.ascontiguousarray(win_q.reshape(P, -1)), "win_k": np.ascontiguousarray(win_k.reshape(P, -1)),
            "pos_t": pos_t}


class Memory:

    def __init__(self, nc, ctx, first_sem, tag):
        self.nc, self.ctx, self.first_sem, self.tag, self.sems = nc, ctx, first_sem, tag, []

    def sb(self, name, shape, dt=F32):
        return self.ctx.enter_context(self.nc.sbuf_tensor(f"{self.tag}_{name}", shape, dt))

    def ps(self, name, shape):
        return self.ctx.enter_context(self.nc.psum_tensor(f"{self.tag}_{name}", shape, F32))

    def sem(self, name):
        s = self.ctx.enter_context(self.nc.semaphore(f"{self.tag}_{name}", num=self.first_sem + len(self.sems)))
        self.sems.append(s)
        return s

    def barrier_and_clear(self):
        nc = self.nc
        first = self.first_sem
        nc.multi_engine_barrier([nc.tensor.engine, nc.vector.engine, nc.scalar.engine, nc.gpsimd.engine,
                                 nc.sync.engine], sems_to_clear=range(first, first + len(self.sems)))


def setup_phase(nc, dram, con, w):
    with ExitStack() as ctx:
        m = Memory(nc, ctx, w["first_sem"], "setup")
        loaded, cb_scaled, cb_turned, done = (m.sem(n) for n in ("loaded", "cb_scaled", "cb_turned", "done"))
        cb = m.sb("cb", [P, KC, C])
        scb = m.sb("scb", [P, KC])
        turned = [m.ps(f"turned{k}", [P, 512]) for k in range(KC)]
        with nc.Block() as block:
            @block.sync
            def _(sp):
                def rows(x):
                    return x.rearrange("(k p) n -> p k n", p=P)
                loads = [(w["qkv_a"][:], rows(dram["w_qkv"])), (w["proj_a"][:], rows(dram["w_proj"])),
                         (w["qkv_b"][:, :, 0:C], rows(dram["Wq"])), (w["qkv_b"][:, :, C:2 * C], rows(dram["Wk"])),
                         (w["qkv_b"][:, :, 2 * C:3 * C], rows(dram["Wv"])), (w["proj_b"][:], rows(dram["Wo"])),
                         (cb[:], rows(dram["CB"])), (scb[:], dram["SCB"].rearrange("(k p) -> p k", p=P)),
                         (w["b_proj"][:], dram["b_proj"].rearrange("(o n) -> o n", o=1).broadcast_to([P, C])),
                         (w["b_ffn"][:], dram["b_ffn"].rearrange("(o n) -> o n", o=1).broadcast_to([P, C])),
                         (w["ident"][:], con["ident"])]
                for dst, src in loads:
                    sp.dma_start(dst, src, allow_slow_non_contiguous=True).then_inc(loaded, 16)
                sp.wait_ge(loaded, 16 * len(loads))

            @block.vector
            def _(dve):
                dve.wait_ge(loaded, 16 * 11)
                for k in range(KC):
                    dve.tensor_scalar(cb[:, k, :], cb[:, k, :], scb[:, k:k + 1], 1.0 / 127.0,
                                      ALU.mult, ALU.mult).then_inc(cb_scaled, 1)
                dve.tensor_copy(w["ident_b"][:], w["ident"][:]).then_inc(done, 1)
                for k in range(KC):
                    dve.wait_ge(cb_turned, k + 1)
                    dve.tensor_copy(w["ffn"][:, k, :], turned[k][:, 0:C]).then_inc(done, 1)

            @block.tensor
            def _(pe):
                pe.wait_ge(loaded, 16 * 11)
                pe.wait_ge(cb_scaled, KC)
                for k in range(KC):
                    for n in range(KC):
                        last = pe.transpose(turned[k][:, n * P:(n + 1) * P], cb[:, n, k * P:(k + 1) * P], w["ident"][:])
                    last.then_inc(cb_turned, 1)
        m.barrier_and_clear()


def token_phase(nc, dram, con, w, scr, tag, src, dst, attn_in, w_proj, b_proj, has_ffn, w_qkv, pos, windows):
    stages = (["turn_a", "project"] if w_proj is not None else []) + (["norm_f", "ffn"] if has_ffn else []) + (
        ["norm_q", "qkv"] if w_qkv is not None else [])
    with ExitStack() as ctx:
        m = Memory(nc, ctx, w["first_sem"], tag)
        X = m.sb("X", [P, NT, C])
        stats = m.sb("stats", [P, TG, 6])
        mv = m.sb("mv", [P, TG, 2])
        var = m.sb("var", [P, TG])
        rstd = m.sb("rstd", [P, TG])
        power = m.sb("power", [P, TG])
        xn = m.sb("xn", [P, 2, TG, C])
        t_bank = [m.ps(f"t_bank{k}", [P, GW]) for k in range(KC)]
        y_bank = [m.ps(f"y_bank{k}", [P, 2, C]) for k in range(2)]
        x_in = [m.sem(f"x_in{g}") for g in range(QG)]
        x_out = m.sem("x_out")
        consts_in, power_set = m.sem("consts_in"), m.sem("power_set")
        stats_done, mv_done, var_done, rstd_done = (m.sem(n) for n in ("stats_done", "mv_done", "var_done", "rstd_done"))
        xn_done, turned, turned_out = m.sem("xn_done"), m.sem("turned"), m.sem("turned_out")
        y_done, y_added, biased = m.sem("y_done"), m.sem("y_added"), m.sem("biased")
        if w_proj is not None:
            at = m.sb("at", [P, NT, C])
            xT_a = m.sb("xT_a", [P, KC, GW])
            at_in = [m.sem(f"at_in{g}") for g in range(QG)]
        if has_ffn:
            xT_f = m.sb("xT_f", [P, KC, GW])
        if w_qkv is not None:
            xT_q = m.sb("xT_q", [P, KC, SP_])
            F = m.sb("F", [P, RING, GW])
            R = m.sb("R", [P, RING, GW])
            parts = m.sb("parts", [P, RING, PARTS, GW], BF16)
            v_rows = m.sb("v_rows", [P, RING, 2, H, VW])
            qk_bank = [m.ps(f"qk_bank{k}", [P, GW]) for k in range(2)]
            v_bank = [m.ps(f"v_bank{k}", [P, 2, C]) for k in range(2)]
            qk_done, f_done, hi_done, rest_done, mid_done, low_done = (
                m.sem(n) for n in ("qk_done", "f_done", "hi_done", "rest_done", "mid_done", "low_done"))
            parts_out = [m.sem(f"parts_out{i}") for i in range(RING)]
            v_done, v_copied = m.sem("v_done"), m.sem("v_copied")
            v_out = [m.sem(f"v_out{i}") for i in range(RING)]
            if pos:
                pos_sb = m.sb("pos", [P, S])
            if windows:
                v_pairs = [[(WQ * u, u) for u in (2 * p, 2 * p + 1)] for p in range(NW // 2)]
                ready = lambda g: [p for p in range(NW // 2) if min(QG - 1, (WQ * (2 * p + 1) + P - PAD - 1) // GW) == g]
            else:
                v_pairs = [[(PAD + P * u, u) for u in (2 * p, 2 * p + 1)] for p in range(NT // 2)]
                ready = lambda g: [p for p in range(NT // 2) if p // (TG // 2) == g]

        with nc.Block() as block:
            @block.vector
            def _(dve):
                n = 1
                dve.memset(power[:], -0.5).then_inc(power_set, 1)
                if w_qkv is not None:
                    dve.memset(xT_q[:, :, 0:PAD], 0.0).then_inc(power_set, 1)
                    dve.memset(xT_q[:, :, PAD + S:SP_], 0.0).then_inc(power_set, 1)
                    dve.memset(v_rows[:], 1.0).then_inc(power_set, 1)
                    n += 3
                dve.wait_ge(power_set, n)
                if pos:
                    dve.wait_ge(consts_in, 16)

            @block.sync
            def _(sp):
                if pos:
                    sp.dma_start(pos_sb[:], con["pos_t"]).then_inc(consts_in, 16)
                    sp.wait_ge(consts_in, 16)
        m.barrier_and_clear()

        def slots():
            for t in range(QG + len(stages) - 1):
                for n in reversed(range(len(stages))):
                    if 0 <= t - n < QG:
                        yield stages[n], t - n

        norms = [s for s in stages if s.startswith("norm")]

        Y = {"project": 2, "ffn": 2}
        TURN = {"turn_a": KC, "norm_f": KC, "norm_q": KC}

        def upto(per, stage, g):
            n = 0
            for s, gg in slots():
                n += per.get(s, 0)
                if (s, gg) == (stage, g):
                    return n

        def biased_by(stage, g):
            if stage == "project":
                return g + 1
            return (QG if b_proj is not None else 0) + upto({"norm_f": 1}, "norm_f", g)

        norm_turned = [upto(TURN, stage, g) for stage, g in slots() if stage in norms]

        @contextmanager
        def batches():
            with nc.Fori(0, B) as b:
                with nc.Block() as block:
                    yield b, block
                m.barrier_and_clear()

        with batches() as (b, block):
            @block.sync
            def _(sp):
                x_src, x_dst = src(b), dst(b) if dst else None
                for g in range(QG):
                    sp.dma_start(X[:, g * TG:(g + 1) * TG, :], x_src[:, g * TG:(g + 1) * TG, :]).then_inc(x_in[g], 16)
                    if w_proj is not None:
                        for h in range(NG):
                            sp.dma_start(at[:, g * TG:(g + 1) * TG, h * HG * D:(h + 1) * HG * D],
                                         attn_in(b, h)[:, g * TG:(g + 1) * TG, :]).then_inc(at_in[g], 16)
                n_qk = n_v = n_y = n_out = 0
                last_add = "ffn" if has_ffn else "project"
                for stage, g in slots():
                    if stage in ("project", "ffn"):
                        n_y += 2
                    if dst and stage == last_add:
                        sp.wait_ge(y_added, n_y)
                        sp.dma_start(x_dst[:, g * TG:(g + 1) * TG, :], X[:, g * TG:(g + 1) * TG, :]).then_inc(x_out, 16)
                        n_out += 1
                    if stage == "qkv":
                        todo = list(ready(g))

                        def store_values(p):
                            nonlocal n_v
                            sp.wait_ge(v_copied, n_v + 1)
                            for i, (_, u) in enumerate(v_pairs[p]):
                                sp.dma_start(scr["v"][b, :, :, u, :].rearrange("h p c -> p h c"),
                                             v_rows[:, n_v % RING, i].rearrange("p (g j) c -> p g (j c)", g=NG)
                                             ).then_inc(v_out[n_v % RING], 16)
                            n_v += 1
                        for i in range(4):
                            if todo:
                                store_values(todo.pop(0))
                            sp.wait_ge(low_done, n_qk + 1)
                            sp.wait_ge(mid_done, n_qk + 1)
                            sp.wait_ge(hi_done, n_qk + 1)
                            for part in range(PARTS):
                                sp.dma_start(
                                    scr["qk"][i // 2][b * 2 + i % 2, :, part, :, g * GW:(g + 1) * GW],
                                    parts[:, n_qk % RING, part, :]).then_inc(parts_out[n_qk % RING], 16)
                            n_qk += 1
                        for p in todo:
                            store_values(p)
                if n_out:
                    sp.wait_ge(x_out, 16 * n_out)
                if n_qk:
                    for i in range(RING):
                        sp.wait_ge(parts_out[i], 16 * PARTS * (n_qk // RING))
                        sp.wait_ge(v_out[i], 32 * (n_v // RING))

            @block.vector
            def _(dve):
                n_norm = n_y = n_qk = 0
                for stage, g in slots():
                    tiles = range(g * TG, (g + 1) * TG)
                    if stage in ("project", "ffn"):
                        if stage == "project" and b_proj is None:
                            dve.wait_ge(x_in[g], 16)
                        else:
                            dve.wait_ge(biased, biased_by(stage, g))
                        for i in range(2):
                            t = g * TG + 2 * i
                            dve.wait_ge(y_done, n_y + 1)
                            dve.tensor_tensor(X[:, t:t + 2, :], y_bank[n_y % 2][:], X[:, t:t + 2, :],
                                              ALU.add).then_inc(y_added, 1)
                            n_y += 1
                    if stage in norms:
                        if stage == stages[0]:
                            dve.wait_ge(x_in[g], 16)
                        else:
                            dve.wait_ge(y_added, upto(Y, {"norm_f": "project", "norm_q": "ffn"}[stage], g))
                        if n_norm:
                            dve.wait_ge(rstd_done, n_norm)
                        for i, t in enumerate(tiles):
                            dve.bn_stats(stats[:, i, :], X[:, t, :]).then_inc(stats_done, 1)
                        dve.wait_ge(stats_done, TG * (n_norm + 1))
                        for i in range(TG):
                            dve.bn_aggr(mv[:, i, :], stats[:, i, :]).then_inc(mv_done, 1)
                        dve.wait_ge(rstd_done, n_norm + 1)
                        dve.wait_ge(mv_done, TG * (n_norm + 1))
                        if n_norm >= 2:
                            dve.wait_ge(turned, norm_turned[n_norm - 2])
                        for i, t in enumerate(tiles):
                            dve.tensor_scalar(xn[:, n_norm % 2, i, :], X[:, t, :], mv[:, i, 0:1], rstd[:, i:i + 1],
                                              ALU.subtract, ALU.mult).then_inc(xn_done, 1)
                        n_norm += 1
                        dve.wait_ge(xn_done, TG * n_norm)
                    if stage == "qkv":
                        def full(n):
                            dve.wait_ge(qk_done, n + 1)
                            if n >= RING:
                                dve.wait_ge(hi_done, n - RING + 1)
                                dve.wait_ge(rest_done, n - RING + 1)
                            if pos:
                                dve.tensor_tensor(F[:, n % RING, :], qk_bank[n % 2][:], pos_sb[:, g * GW:(g + 1) * GW],
                                                  ALU.add).then_inc(f_done, 1)
                            else:
                                dve.tensor_copy(F[:, n % RING, :], qk_bank[n % 2][:]).then_inc(f_done, 1)

                        def rest(n):
                            dve.wait_ge(f_done, n + 1)
                            dve.wait_ge(hi_done, n + 1)
                            if n >= RING:
                                dve.wait_ge(mid_done, n - RING + 1)
                                dve.wait_ge(low_done, n - RING + 1)
                            dve.tensor_tensor(R[:, n % RING, :], F[:, n % RING, :], parts[:, n % RING, 0, :],
                                              ALU.subtract).then_inc(rest_done, 1)
                        for i in range(4):
                            full(n_qk + i)
                            if i >= 2:
                                rest(n_qk + i - 2)
                        rest(n_qk + 2)
                        rest(n_qk + 3)
                        n_qk += 4

            @block.gpsimd
            def _(pool):
                n_norm = 0
                if b_proj is not None:
                    for g in range(QG):
                        pool.wait_ge(x_in[g], 16)
                        for t in range(g * TG, (g + 1) * TG):
                            last = pool.tensor_tensor(X[:, t, :], X[:, t, :], w[b_proj][:], ALU.add)
                        last.then_inc(biased, 1)
                n_qk = 0
                for stage, g in slots():
                    if stage in norms:
                        pool.wait_ge(mv_done, TG * (n_norm + 1))
                        if n_norm:
                            pool.wait_ge(xn_done, TG * n_norm)
                        pool.tensor_scalar(var[:], mv[:, :, 1], EPS, None, ALU.add).then_inc(var_done, 1)
                        pool.wait_ge(var_done, n_norm + 1)
                        pool.tensor_tensor(rstd[:], var[:], power[:], ALU.pow).then_inc(rstd_done, 1)
                        n_norm += 1
                        if stage == "norm_f":
                            pool.wait_ge(xn_done, TG * n_norm)
                            for t in range(g * TG, (g + 1) * TG):
                                last = pool.tensor_tensor(X[:, t, :], X[:, t, :], w["b_ffn"][:], ALU.add)
                            last.then_inc(biased, 1)
                    if stage == "qkv":
                        for i in range(4):
                            pool.wait_ge(rest_done, n_qk + 1)
                            pool.wait_ge(mid_done, n_qk + 1)
                            if n_qk >= RING:
                                pool.wait_ge(parts_out[n_qk % RING], 16 * PARTS * (n_qk // RING))
                            pool.tensor_tensor(parts[:, n_qk % RING, 2, :], R[:, n_qk % RING, :], parts[:, n_qk % RING, 1, :],
                                               ALU.subtract).then_inc(low_done, 1)
                            n_qk += 1

            @block.scalar
            def _(act):
                n_turn = n_qk = n_v = 0
                for stage, g in slots():
                    if stage in TURN:
                        for k in range(KC):
                            act.wait_ge(turned, n_turn + 1)
                            if stage == "turn_a":
                                if g >= 1:
                                    act.wait_ge(y_done, upto(Y, "project", g - 1))
                                out = xT_a[:, k, :]
                            elif stage == "norm_f":
                                if g >= 1:
                                    act.wait_ge(y_done, upto(Y, "ffn", g - 1))
                                out = xT_f[:, k, :]
                            else:
                                out = xT_q[:, k, PAD + g * GW:PAD + (g + 1) * GW]
                            act.activation(out, t_bank[k][:], ACT.Copy).then_inc(turned_out, 1)
                            n_turn += 1
                    if stage == "qkv":
                        def hi(n):
                            act.wait_ge(f_done, n + 1)
                            if n >= RING:
                                act.wait_ge(parts_out[n % RING], 16 * PARTS * (n // RING))
                            act.activation(parts[:, n % RING, 0, :], F[:, n % RING, :], ACT.Copy).then_inc(hi_done, 1)

                        def mid(n):
                            act.wait_ge(rest_done, n + 1)
                            act.activation(parts[:, n % RING, 1, :], R[:, n % RING, :], ACT.Copy).then_inc(mid_done, 1)

                        def values(p):
                            nonlocal n_v
                            act.wait_ge(v_done, n_v + 1)
                            if n_v >= RING:
                                act.wait_ge(v_out[n_v % RING], 32 * (n_v // RING))
                            act.activation(v_rows[:, n_v % RING, :, :, 0:D],
                                           v_bank[n_v % 2][:].rearrange("p u (h d) -> p u h d", h=H),
                                           ACT.Copy).then_inc(v_copied, 1)
                            n_v += 1
                        todo = list(ready(g))
                        for i in range(4):
                            hi(n_qk + i)
                            if i >= 2:
                                mid(n_qk + i - 2)
                            if todo:
                                values(todo.pop(0))
                        mid(n_qk + 2)
                        mid(n_qk + 3)
                        n_qk += 4
                        for p in todo:
                            values(p)

            @block.tensor
            def _(pe):
                n_norm = n_turn = n_y = n_qk = n_v = 0

                def rows_product(n, lhs, weights):
                    for i in range(2):
                        for k in range(KC):
                            last = pe.matmul(y_bank[n % 2][:, i, :], lhs(i, k), weights[:, k, :],
                                             start=(k == 0), stop=(k == KC - 1))
                    last.then_inc(y_done, 1)

                for stage, g in slots():
                    if stage == "project":
                        pe.wait_ge(turned_out, upto(TURN, "turn_a", g))
                        for i in range(2):
                            if n_y >= 2:
                                pe.wait_ge(y_added, n_y - 1)
                            c0 = 2 * i * P
                            rows_product(n_y, lambda t, k: xT_a[:, k, c0 + t * P:c0 + (t + 1) * P], w[w_proj])
                            n_y += 1
                    if stage == "ffn":
                        pe.wait_ge(turned_out, upto(TURN, "norm_f", g))
                        for i in range(2):
                            if n_y >= 2:
                                pe.wait_ge(y_added, n_y - 1)
                            c0 = 2 * i * P
                            rows_product(n_y, lambda t, k: xT_f[:, k, c0 + t * P:c0 + (t + 1) * P], w["ffn"])
                            n_y += 1
                    if stage in TURN:
                        if stage == "turn_a":
                            pe.wait_ge(at_in[g], 16 * NG)
                        else:
                            pe.wait_ge(xn_done, TG * (n_norm + 1))
                        for k in range(KC):
                            if n_turn >= KC:
                                pe.wait_ge(turned_out, n_turn - KC + 1)
                            for i in range(TG):
                                if stage == "turn_a":
                                    rows = at[:, g * TG + i, k * P:(k + 1) * P]
                                else:
                                    rows = xn[:, n_norm % 2, i, k * P:(k + 1) * P]
                                last = pe.transpose(t_bank[k][:, i * P:(i + 1) * P], rows, w["ident"][:])
                            last.then_inc(turned, 1)
                            n_turn += 1
                        n_norm += stage != "turn_a"
                    if stage == "qkv":
                        pe.wait_ge(turned_out, upto(TURN, "norm_q", g))

                        def values(p):
                            nonlocal n_v
                            if n_v >= 2:
                                pe.wait_ge(v_copied, n_v - 1)
                            for i, (c0, _) in enumerate(v_pairs[p]):
                                for k in range(KC):
                                    last = pe.matmul(v_bank[n_v % 2][:, i, :], xT_q[:, k, c0:c0 + P],
                                                     w[w_qkv][:, k, 2 * C:3 * C], start=(k == 0), stop=(k == KC - 1))
                            last.then_inc(v_done, 1)
                            n_v += 1
                        todo = list(ready(g))
                        for i in range(4):
                            if n_qk >= 2:
                                pe.wait_ge(f_done, n_qk - 1)
                            for k in range(KC):
                                last = pe.matmul(qk_bank[n_qk % 2][:], w[w_qkv][:, k, i * P:(i + 1) * P],
                                                 xT_q[:, k, PAD + g * GW:PAD + (g + 1) * GW],
                                                 start=(k == 0), stop=(k == KC - 1))
                            last.then_inc(qk_done, 1)
                            n_qk += 1
                            if todo:
                                values(todo.pop(0))
                        for p in todo:
                            values(p)



def attention_phase(nc, con, w, scr, tag, windows, score_scale):
    KW = P + 2 * WIN
    QT = NT
    if windows:
        units = [(g, None, None, 0) for g in range(QG)]
    else:
        units = [(g, kb, kb, max(0, kb - TG * g) * P) for g in range(QG) for kb in range(TG * (g + 1))]
    U = len(units)
    last_unit = {g: max(u for u in range(U) if units[u][0] == g) for g in range(QG)}
    if windows:
        jobs = [(g, j, t, 0, 2 * KW) for g in range(QG) for t in range(g * TG, (g + 1) * TG, 2) for j in range(HG)]
    else:
        jobs = [(t // TG, j, t, c, min(GW, (t + 1) * P - c * GW))
                for t in range(QT) for j in range(HG) for c in range(t // TG + 1)]
    weight = [sum(GW - x[3] for x in units[:u + 1]) for u in range(U)]
    cols = [sum(x[4] for x in jobs[:i + 1]) for i in range(len(jobs))]
    unit_of = [min(u for u in range(U) if cols[i] * weight[-1] <= weight[u] * cols[-1] + 1) for i in range(len(jobs))]
    jobs_at = [[i for i in range(len(jobs)) if unit_of[i] == u] for u in range(U)]
    group_jobs = [sum(1 for x in jobs if x[0] <= g) for g in range(QG)]
    max_end = [unit_of[group_jobs[g] - 1] for g in range(QG)]

    with ExitStack() as ctx:
        m = Memory(nc, ctx, w["first_sem"], tag)
        QA = m.sb("QA", [P, BUFS, HG, SP_], BF16)
        KA = m.sb("KA", [P, BUFS, HG, SP_], BF16)
        VT = NW if windows else NT
        V = m.sb("V", [P, BUFS, VT, HG, VW])
        probs = m.sb("probs", [P, 2, HG, GW])
        o_sb = m.sb("o_sb", [P, 2, GW])
        inv = m.sb("inv", [P, TG, HG])
        o_norm = m.sb("o_norm", [P, 2, TG, HG, D])
        part = m.sb("part", [P, HG, QT, QG])
        top = m.sb("top", [P, QG, HG, TG])
        low = m.sb("low", [HG * TG, P])
        rest = m.sb("rest", [HG * TG, P])
        low_parts = m.sb("low_parts", [HG * TG, 2, PARTS, P], BF16)
        if windows:
            mask_f = m.sb("mask_f", [P, 3 * GW])
            mask_k = m.sb("mask_k", [P, 3, GW], BF16)
            mask_q = m.sb("mask_q", [P, 3, 2 * KW], BF16)
        else:
            mask_f = m.sb("mask_f", [P, P])
            mask_k = m.sb("mask_k", [P, P], BF16)
            mask_q = m.sb("mask_q", [P, GW])
            junk = m.sb("junk", [P, 2, GW], BF16)
        s_bank = m.ps("s_bank", [P, 2, 2, GW])
        m_bank = [m.ps(f"m_bank{i}", [P, GW]) for i in range(2)]
        o_bank = m.ps("o_bank", [P, GW])
        x_bank = m.ps("x_bank", [P, GW])

        setup, set_in = m.sem("setup"), m.sem("set_in")
        qk_in = [m.sem(f"qk_in{k}") for k in range(BUFS)]
        v_in = [m.sem(f"v_in{k}") for k in range(BUFS)]
        low_kept = m.sem("low_kept")
        low_in = [[m.sem(f"low_in{k}{g}") for g in range(QG)] for k in range(BUFS)]
        out_done = [m.sem(f"out_done{i}") for i in range(2)]
        s_done, exp_done, pv_done = m.sem("s_done"), m.sem("exp_done"), m.sem("pv_done")
        m_done, m_free, part_done, top_done = m.sem("m_done"), m.sem("m_free"), m.sem("part_done"), m.sem("top_done")
        top_turned, low_done, split_1, split_2, split_3, split_4 = (
            m.sem(n) for n in ("top_turned", "low_done", "split_1", "split_2", "split_3", "split_4"))
        o_copied, o_turned, inv_done, norm_done = (m.sem(n) for n in ("o_copied", "o_turned", "inv_done", "norm_done"))

        def load(sp, step, buf, arrived):
            for blocks, dst, which in ((Q_BLOCKS, QA, 0), (K_BLOCKS, KA, 1)):
                for first, n, row in blocks:
                    src = scr["qk"][which].rearrange("o h p d s -> (o h) (p d) s")
                    src = src[bass.ds(step * HG, HG), first * D:(first + n) * D, :]
                    sp.dma_start(dst[row * D:(row + n) * D, buf, :, PAD:PAD + S],
                                 src.rearrange("j r s -> r j s")).then_inc(arrived, 16)

        def load_v(sp, step, buf, arrived):
            src = scr["v"].rearrange("b g p u c -> (b g) p u c")[bass.ds(step, 1)]
            sp.dma_start(V[:, buf].rearrange("p u j c -> p (u j c)"),
                         src.rearrange("o p u c -> (o p) (u c)")).then_inc(arrived, 16)

        with nc.Block() as block:
            @block.sync
            def _(sp):
                if windows:
                    sp.dma_start(mask_f[:, 0:3 * GW], con["win_k"]).then_inc(set_in, 16)
                    sp.wait_ge(setup, 1)
                    sp.dma_start(mask_f[:, 0:6 * KW], con["win_q"]).then_inc(set_in, 16)
                    sp.wait_ge(set_in, 32)
                else:
                    sp.dma_start(mask_f[:], con["causal_kq"]).then_inc(set_in, 16)
                    sp.dma_start(mask_q[:], con["causal_q"]).then_inc(set_in, 16)
                    sp.wait_ge(set_in, 32)

            @block.vector
            def _(dve):
                if windows:
                    dve.wait_ge(set_in, 16)
                    dve.tensor_copy(mask_k[:].rearrange("p a n -> p (a n)"), mask_f[:]).then_inc(setup, 1)
                    dve.wait_ge(set_in, 32)
                    dve.tensor_copy(mask_q[:].rearrange("p a n -> p (a n)"), mask_f[:, 0:6 * KW]).then_inc(setup, 1)
                else:
                    dve.wait_ge(set_in, 32)
                    dve.tensor_copy(mask_k[:], mask_f[:]).then_inc(setup, 1)
                    dve.memset(junk[:], 0.0).then_inc(setup, 1)
                dve.memset(part[:], LOWEST).then_inc(setup, 1)
                dve.memset(o_bank[:], 0.0).then_inc(setup, 1)
                dve.wait_ge(setup, 4)

            @block.gpsimd
            def _(pool):
                for X in (QA, KA):
                    pool.memset(X[:, :, :, 0:PAD], 0.0).then_inc(low_done, 1)
                    pool.memset(X[:, :, :, PAD + S:SP_], 0.0).then_inc(low_done, 1)
                pool.wait_ge(low_done, 4)
                pool.memset(KA[ROWS:ROWS + PARTS], 1.0).then_inc(low_done, 1)
                pool.wait_ge(low_done, 5)
        m.barrier_and_clear()

        def part_of_program(steps, loads, block, exp=True, first_max=0):
            K = len(steps)
            has_max = [not (exp and k == K - 1 and first_max < 0) for k in range(K)]
            NU = U if exp else U
            exp_buf = [k % BUFS for k in range(K)]
            max_buf = [(k + (1 if exp else 0)) % BUFS for k in range(K)]

            def x_uses(k):
                uses = []
                for u in range(U + 2):
                    for g in range(QG):
                        if exp and last_unit[g] + 2 == u:
                            uses.append((u, "sum", g))
                        if has_max[k] and max_end[g] + 1 == u:
                            uses.append((u, "top", g))
                return uses
            uses = [(k, *x) for k in range(K) for x in x_uses(k)]

            def uses_before(k, u, kind, g):
                i = uses.index((k, u, kind, g))
                return (sum(1 for x in uses[:i] if x[2] == "sum"), sum(1 for x in uses[:i] if x[2] == "top"),
                        uses[i - 1][2] if i else None)

            @block.sync
            def _(sp):
                n_low = n_out = 0
                for k in range(K):
                    if loads[k] is not None:
                        if exp and k:
                            sp.wait_ge(pv_done, k * U)
                        (qk_step, qk_buf), (v_step, v_buf) = loads[k]
                        load(sp, qk_step, qk_buf, qk_in[k])
                        load_v(sp, v_step, v_buf, v_in[k])
                    for u in range(U + 2):
                        for g in range(QG):
                            if has_max[k] and max_end[g] + 1 == u:
                                sp.wait_ge(split_4, n_low + 1)
                                kept = scr["low"][n_low % (BUFS * QG)]
                                sp.dma_start(kept.rearrange("r j (t q) -> (j t) r q", t=TG),
                                             low_parts[:, n_low % 2]).then_inc(low_kept, 16)
                                sp.wait_ge(low_kept, 16 * (n_low + 1))
                                sp.dma_start(QA[ROWS:ROWS + PARTS, max_buf[k], :, PAD + g * GW:PAD + (g + 1) * GW],
                                             kept).then_inc(low_in[k][g], 16)
                                n_low += 1
                            if exp and last_unit[g] + 2 == u:
                                sp.wait_ge(norm_done, n_out + 1)
                                dst = scr["attn"][bass.ds(steps[k], 1), :, g * TG:(g + 1) * TG, :]
                                sp.dma_start(dst.rearrange("o p t c -> (o p) (t c)"),
                                             o_norm[:, n_out % 2].rearrange("p t j d -> p (t j d)")
                                             ).then_inc(out_done[n_out % 2], 16)
                                n_out += 1
                for k in range(K):
                    if loads[k] is not None:
                        sp.wait_ge(qk_in[k], 16 * ROW_LOADS)
                        sp.wait_ge(v_in[k], 16)
                    if has_max[k]:
                        for g in range(QG):
                            sp.wait_ge(low_in[k][g], 16)
                if exp:
                    for i in range(2):
                        sp.wait_ge(out_done[i], 16 * (n_out // 2))

            @block.tensor
            def _(pe):
                n_job = n_half = n_pv = 0

                def scores(k, u, half):
                    nonlocal n_half
                    g, kb, _, off = units[u]
                    buf = exp_buf[k]
                    if half == 0 and k and u == last_unit.get(g - 1, -1) + 1:
                        pe.wait_ge(low_in[k - 1][g], 16)
                    if n_half >= 2:
                        pe.wait_ge(exp_done, n_half - 1)
                    for i in range(2):
                        j = 2 * half + i
                        bank = s_bank[:, n_half % 2, i, :]
                        if windows:
                            v = 0 if g == 0 else 2 if g == QG - 1 else 1
                            pe.matmul(bank, w["ident_b"][:], mask_k[:, v, :], start=True, stop=False)
                            for n in range(GW // WQ):
                                q0 = g * GW + n * WQ
                                last = pe.matmul(bank[:, n * WQ:(n + 1) * WQ], KA[0:ROWS + PARTS, buf, j, q0:q0 + P],
                                                 QA[0:ROWS + PARTS, buf, j, PAD + q0:PAD + q0 + WQ],
                                                 start=False, stop=(n == GW // WQ - 1))
                        else:
                            diag = kb >= TG * g
                            last = pe.matmul(bank[:, off:GW], KA[0:ROWS + PARTS, buf, j, PAD + kb * P:PAD + (kb + 1) * P],
                                             QA[0:ROWS + PARTS, buf, j, PAD + g * GW + off:PAD + (g + 1) * GW],
                                             start=True, stop=not diag)
                            if diag:
                                last = pe.matmul(bank[:, off:off + P], w["ident_b"][:], mask_k[:],
                                                 start=False, stop=True)
                    last.then_inc(s_done, 1)
                    n_half += 1

                def values(k, u):
                    nonlocal n_pv
                    g, kb, _, off = units[u]
                    buf = exp_buf[k]
                    pe.wait_ge(exp_done, 2 * n_pv + 2)
                    if u == 0 and k:
                        pe.wait_ge(v_in[k - 1], 16)
                    first = u == last_unit.get(g - 1, -1) + 1
                    if first and k * QG + g:
                        pe.wait_ge(o_copied, k * QG + g)
                    if windows:
                        for n in range(GW // WQ):
                            for j in range(HG):
                                last = pe.matmul(o_bank[32 * j:32 * j + VW, n * WQ:(n + 1) * WQ],
                                                 V[:, buf, g * (GW // WQ) + n, j, :],
                                                 probs[:, n_pv % 2, j, n * WQ:(n + 1) * WQ], start=True, stop=True)
                    else:
                        for j in range(HG):
                            last = pe.matmul(o_bank[32 * j:32 * j + VW, off:GW], V[:, buf, kb, j, :],
                                             probs[:, n_pv % 2, j, off:GW], start=first, stop=(u == last_unit[g]))
                    last.then_inc(pv_done, 1)
                    n_pv += 1

                def maxima(k, i):
                    nonlocal n_job
                    g, j, t, c, n = jobs[i]
                    buf = max_buf[k]
                    if n_job >= 2:
                        pe.wait_ge(m_free, n_job - 1)
                    bank = m_bank[n_job % 2]
                    q_tile = lambda t: QA[0:ROWS, buf, j, PAD + t * P:PAD + (t + 1) * P]
                    if windows:
                        v = 0 if t == 0 else 2 if t == QT - 2 else 1
                        pe.matmul(bank[:, 0:n], w["ident_b"][:], mask_q[:, v, :], start=True, stop=False)
                        for x in range(2):
                            last = pe.matmul(bank[:, x * KW:(x + 1) * KW], q_tile(t + x),
                                             KA[0:ROWS, buf, j, (t + x) * P:(t + x) * P + KW], start=False, stop=(x == 1))
                    else:
                        last = pe.matmul(bank[:, 0:n], q_tile(t), KA[0:ROWS, buf, j, PAD + c * GW:PAD + c * GW + n],
                                         start=True, stop=True)
                    last.then_inc(m_done, 1)
                    n_job += 1

                def take_x_bank(k, u, kind, g):
                    sums, tops, before = uses_before(k, u, kind, g)
                    if before == "sum":
                        pe.wait_ge(norm_done, sums)
                    if before == "top":
                        pe.wait_ge(low_done, tops)

                for k in range(K):
                    if has_max[k] and exp and k:
                        pe.wait_ge(qk_in[k - 1], 16 * ROW_LOADS)
                    for u in range(U + 2):
                        todo = jobs_at[u] if has_max[k] and u < U else []
                        quarter = len(todo) // 4
                        if exp and u < U:
                            scores(k, u, 0)
                        for i in todo[:quarter]:
                            maxima(k, i)
                        if exp and u < U:
                            scores(k, u, 1)
                        for i in todo[quarter:2 * quarter]:
                            maxima(k, i)
                        if exp and 1 <= u <= U:
                            values(k, u - 1)
                        for i in todo[2 * quarter:]:
                            maxima(k, i)
                        for g in range(QG):
                            if exp and last_unit[g] + 2 == u:
                                take_x_bank(k, u, "sum", g)
                                pe.wait_ge(o_copied, k * QG + g + 1)
                                for t in range(TG):
                                    last = pe.transpose(x_bank[:, t * P:(t + 1) * P],
                                                        o_sb[:, (k * QG + g) % 2, t * P:(t + 1) * P], w["ident"][:])
                                last.then_inc(o_turned, 1)
                            if has_max[k] and max_end[g] + 1 == u:
                                take_x_bank(k, u, "top", g)
                                pe.wait_ge(top_done, k * QG + g + 1)
                                pe.transpose(x_bank[0:HG * TG, 0:P], top[:, g].rearrange("p j t -> p (j t)"),
                                             w["ident"][:]).then_inc(top_turned, 1)

            @block.scalar
            def _(act):
                n_half = n_pv = 0
                for k in range(K):
                    for u in range(U + 2):
                        if exp and u < U:
                            off = units[u][3]
                            for half in range(2):
                                act.wait_ge(s_done, n_half + 1)
                                if n_pv >= 2 and half == 0:
                                    act.wait_ge(pv_done, n_pv - 1)
                                act.activation(probs[:, n_pv % 2, 2 * half:2 * half + 2, off:GW],
                                               s_bank[:, n_half % 2, :, off:GW], ACT.Exp,
                                               scale=score_scale).then_inc(exp_done, 1)
                                n_half += 1
                            n_pv += 1
                        for g in range(QG):
                            if exp and last_unit[g] + 1 == u:
                                n = k * QG + g
                                act.wait_ge(pv_done, k * U + last_unit[g] + 1)
                                if n >= 2:
                                    act.wait_ge(o_turned, n - 1)
                                act.activation(o_sb[:, n % 2, :], o_bank[:], ACT.Copy).then_inc(o_copied, 1)
                            if has_max[k] and max_end[g] + 1 == u:
                                n = k * QG + g
                                act.wait_ge(top_turned, n + 1)
                                if n >= 1:
                                    act.wait_ge(split_2, n)
                                act.activation(low[:], x_bank[0:HG * TG, 0:P], ACT.Copy, scale=-1.0).then_inc(low_done, 1)

            @block.vector
            def _(dve):
                n_job = 0
                for k in range(K):
                    for u in range(U + 3):
                        if has_max[k] and u < U:
                            for i in jobs_at[u]:
                                g, j, t, c, n = jobs[i]
                                bank = m_bank[n_job % 2]
                                dve.wait_ge(m_done, n_job + 1)
                                if windows:
                                    ins = dve.tensor_reduce(part[:, j, t:t + 2, 0], bank[:, 0:2 * KW].rearrange(
                                        "p (x n) -> p x n", x=2), AX, ALU.max)
                                elif c == t // TG:
                                    if n_job >= 2:
                                        dve.wait_ge(m_free, n_job - 1)
                                    ins = dve.tensor_tensor_reduce(junk[:, n_job % 2, 0:n], bank[:, 0:n], mask_q[:, GW - n:GW], 1.0,
                                                                   LOWEST, ALU.add, ALU.max, part[:, j, t, c:c + 1])
                                else:
                                    ins = dve.tensor_reduce(part[:, j, t, c:c + 1], bank[:, 0:n], AX, ALU.max)
                                ins.then_inc(m_free, 1)
                                n_job += 1
                                if group_jobs[g] == i + 1:
                                    dve.wait_ge(m_free, n_job)
                                    if k:
                                        dve.wait_ge(top_turned, (k - 1) * QG + g + 1)
                                    dve.tensor_reduce(top[:, g], part[:, :, g * TG:(g + 1) * TG, :], AX,
                                                      ALU.max).then_inc(top_done, 1)
                        for g in range(QG):
                            if exp and last_unit[g] + 2 == u:
                                n = k * QG + g
                                rows = x_bank[:].rearrange("p (t j r) -> p t j r", t=TG, j=HG)
                                dve.wait_ge(o_turned, n + 1)
                                dve.reciprocal(inv[:], rows[:, :, :, D]).then_inc(inv_done, 1)
                                dve.wait_ge(inv_done, n + 1)
                                if n >= 2:
                                    dve.wait_ge(out_done[n % 2], 16 * (n // 2))
                                dve.tensor_tensor(o_norm[:, n % 2], rows[:, :, :, 0:D],
                                                  inv[:].unsqueeze(3).broadcast_to([P, TG, HG, D]),
                                                  ALU.mult).then_inc(norm_done, 1)

            @block.gpsimd
            def _(pool):
                for k in range(K):
                    for u in range(U + 2):
                        for g in range(QG):
                            n = k * QG + g
                            if has_max[k] and max_end[g] + 1 == u:
                                half = low_parts[:, n % 2]
                                pool.wait_ge(low_done, n + 1)
                                if n >= 2:
                                    pool.wait_ge(low_kept, 16 * (n - 1))
                                pool.tensor_copy(half[:, 0, :], low[:]).then_inc(split_1, 1)
                                pool.wait_ge(split_1, n + 1)
                                pool.tensor_tensor(rest[:], low[:], half[:, 0, :], ALU.subtract).then_inc(split_2, 1)
                                pool.wait_ge(split_2, n + 1)
                                pool.tensor_copy(half[:, 1, :], rest[:]).then_inc(split_3, 1)
                                pool.wait_ge(split_3, n + 1)
                                pool.tensor_tensor(half[:, 2, :], rest[:], half[:, 1, :],
                                                   ALU.subtract).then_inc(split_4, 1)

        with nc.Block() as block:
            @block.sync
            def _(sp):
                for n in range(2):
                    load(sp, n, n, qk_in[n])
                load_v(sp, 0, 0, v_in[0])
                for n in range(2):
                    sp.wait_ge(qk_in[n], 16 * ROW_LOADS)
                sp.wait_ge(v_in[0], 16)
        m.barrier_and_clear()
        with nc.Block() as block:
            part_of_program([0], [None], block, exp=False)
        m.barrier_and_clear()
        with nc.Fori(0, LOOPS) as i:
            with nc.Block() as block:
                part_of_program([BUFS * i + k for k in range(BUFS)],
                                [(((BUFS * i + k + 2) % STEPS, (k + 2) % BUFS), (BUFS * i + k + 1, (k + 1) % BUFS))
                                 for k in range(BUFS)], block)
            m.barrier_and_clear()
        with nc.Block() as block:
            part_of_program([STEPS - 1], [None], block, first_max=-1)
        m.barrier_and_clear()


def program(nc, dram, con, out):
    with ExitStack() as ctx:
        def sb(name, shape, dt=F32):
            return ctx.enter_context(nc.sbuf_tensor(name, shape, dt))
        with nc.semaphore("lowest_free") as lowest:
            first_sem = lowest.num
        w = {"first_sem": first_sem, "qkv_a": sb("qkv_a", [P, KC, 3 * C]), "qkv_b": sb("qkv_b", [P, KC, 3 * C]),
             "proj_a": sb("proj_a", [P, KC, C]), "proj_b": sb("proj_b", [P, KC, C]), "ffn": sb("ffn", [P, KC, C]),
             "b_proj": sb("b_proj", [P, C]), "b_ffn": sb("b_ffn", [P, C]),
             "ident": sb("ident", [P, P]), "ident_b": sb("ident_b", [P, P], BF16)}
        x2 = nc.dram_tensor("x2", (B, S, C), F32, kind="Internal").ap()
        qk = [nc.dram_tensor(n, (B * 2, H // 2, PARTS, D, S), BF16, kind="Internal").ap() for n in ("q_parts", "k_parts")]
        v_w = nc.dram_tensor("v_w", (B, NG, P, NW, HG * VW), F32, kind="Internal").ap()
        v_t = nc.dram_tensor("v_t", (B, NG, P, NT, HG * VW), F32, kind="Internal").ap()
        low = nc.dram_tensor("low_maxima", (BUFS * QG, PARTS, HG, GW), BF16, kind="Internal").ap()
        attn = nc.dram_tensor("attn", (STEPS, P, NT, HG * D), F32, kind="Internal").ap()

        def rows(x):
            return lambda b: x[bass.ds(b, 1)].rearrange("o (t p) c -> p (o t) c", p=P)

        def attn_in(b, h):
            return attn[bass.ds(b * NG + h, 1)].rearrange("h p t c -> (h p) t c")
        setup_phase(nc, dram, con, w)
        token_phase(nc, dram, con, w, {"qk": qk, "v": v_w}, "first", rows(dram["x"]), None, None, None, None, False,
                    "qkv_a", False, True)
        attention_phase(nc, con, w, {"qk": qk, "v": v_w, "attn": attn, "low": low}, "window", True, D ** -0.5)
        token_phase(nc, dram, con, w, {"qk": qk, "v": v_t}, "middle", rows(dram["x"]), rows(x2), attn_in, "proj_a", "b_proj",
                    True, "qkv_b", True, False)
        attention_phase(nc, con, w, {"qk": qk, "v": v_t, "attn": attn, "low": low}, "causal", False, C ** -0.5)
        token_phase(nc, dram, con, w, None, "last", rows(x2), rows(out), attn_in, "proj_b", None, True, None, False, False)


_INS = {"x": "L0_attn_a_x", "w_qkv": "L0_attn_a_w_qkv", "w_proj": "L0_attn_a_w_proj", "b_proj": "L0_attn_a_b_proj",
        "Wq": "L0_attn_b_Wq", "Wk": "L0_attn_b_Wk", "Wv": "L0_attn_b_Wv", "Wo": "L0_attn_b_Wo",
        "CB": "L0_ffn_CB", "SCB": "L0_ffn_SCB", "b_ffn": "L0_ffn_bias"}


def kernel(**inputs):
    import numpy as _np
    import concourse.bacc as _bacc
    from concourse import mybir as _mybir
    from concourse.bass_utils import run_bass_kernel_spmd as _run

    nc = _bacc.Bacc("TRN2", target_bir_lowering=False, num_devices=1)
    arrays, dram, con = {}, {}, {}
    for short, name in _INS.items():
        a = _np.ascontiguousarray(inputs[name])
        arrays[f"in_{short}"] = a
        dram[short] = nc.dram_tensor(f"in_{short}", a.shape, _mybir.dt.from_np(a.dtype), kind="ExternalInput").ap()
    for name, a in constants().items():
        arrays[f"const_{name}"] = a
        con[name] = nc.dram_tensor(f"const_{name}", a.shape, _mybir.dt.from_np(a.dtype), kind="ExternalInput").ap()
    out = nc.dram_tensor("out_dram", (B, S, C), F32, kind="ExternalOutput").ap()
    program(nc, dram, con, out)
    r = _run(nc, [arrays], core_ids=[0])
    return r.results[0]["out_dram"]
```

```python
from contextlib import ExitStack, contextmanager

import numpy as np
import concourse.bass as bass
from concourse import mybir

F32 = mybir.dt.float32
BF16 = mybir.dt.bfloat16
F32R = mybir.dt.float32r
ALU = mybir.AluOpType
ACT = mybir.ActivationFunctionType
AX = mybir.AxisListType.X

P = 128
B, S, C = 4, 2048, 256
H, D = 16, 16
HG = 4
NG = H // HG
STEPS = B * NG
KC = C // P
QG = 4
GW = S // QG
TG = GW // P
NT = S // P
WIN = 32
WQ = 64
NW = S // WQ
PAD = WIN
SP_ = S + 2 * PAD
BATCHES = 2
M_RING = 3
INV_RING = 4
RING = 4
PARTS = 3
ROWS = 6 * D
VW = D + 1
NEG = -1e30
LOWEST = -3e38
EPS = 1e-5
LOWS = 4
BUFS = 3
LOOPS = (STEPS - 1) // BUFS

Q_BLOCKS = [0, 1, 0, 1, 2, 0]
K_BLOCKS = [0, 0, 1, 1, 0, 2]
ROW_LOADS = len(Q_BLOCKS) + len(K_BLOCKS)


UPPER, LOWER = 0, 1
TERMS = [(UPPER, UPPER), (UPPER, LOWER), (LOWER, UPPER)]
PRODUCTS = [(k, *x) for k in range(KC) for x in TERMS]


def constants():
    f = np.float32
    ident = np.eye(P, dtype=f)
    k, q = np.arange(P)[:, None], np.arange(P)[None, :]
    causal_kq = np.where(k > q, NEG, 0.0).astype(f)
    causal_q = np.zeros((P, GW), f)
    causal_q[:, GW - P:] = causal_kq.T
    kk = np.arange(P + 2 * WIN)[None, :]
    qq = np.arange(P)[:, None]
    mid = (kk - qq >= 0) & (kk - qq <= 2 * WIN)
    first, last = mid & (kk >= WIN), mid & (kk < P + WIN)
    win_q = np.stack([np.concatenate([first, mid], 1), np.concatenate([mid, mid], 1),
                      np.concatenate([mid, last], 1)], 1)
    win_q = np.where(win_q, 0.0, NEG).astype(f)
    qq = np.arange(WQ)[None, :]
    mid = (k - qq >= 0) & (k - qq <= 2 * WIN)
    first, last = mid & (k >= WIN), mid & (k < P - WIN)
    n = GW // WQ
    win_k = np.stack([np.concatenate([first] + [mid] * (n - 1), 1), np.concatenate([mid] * n, 1),
                      np.concatenate([mid] * (n - 1) + [last], 1)], 1)
    win_k = np.where(win_k, 0.0, NEG).astype(f)
    idx = np.arange(S, dtype=f)
    scale = (f(1.0) / (np.power(f(10000.0), np.arange(0, D, 2, dtype=f) / f(D)) + np.finfo(f).eps)).astype(f)
    ang = (idx[:, None] * scale[None, :]).astype(f)
    pos = np.stack([np.sin(ang), np.cos(ang)], -1).reshape(S, D).astype(f)
    pos_t = np.ascontiguousarray(np.tile(pos.T, (P // D, 1)))
    return {"ident": ident, "causal_kq": causal_kq, "causal_q": causal_q,
            "win_q": np.ascontiguousarray(win_q.reshape(P, -1)), "win_k": np.ascontiguousarray(win_k.reshape(P, -1)),
            "pos_t": pos_t}


class Memory:

    def __init__(self, nc, ctx, first_sem, tag):
        self.nc, self.ctx, self.first_sem, self.tag, self.sems = nc, ctx, first_sem, tag, []

    def sb(self, name, shape, dt=F32):
        return self.ctx.enter_context(self.nc.sbuf_tensor(f"{self.tag}_{name}", shape, dt))

    def ps(self, name, shape):
        return self.ctx.enter_context(self.nc.psum_tensor(f"{self.tag}_{name}", shape, F32))

    def sem(self, name):
        s = self.ctx.enter_context(self.nc.semaphore(f"{self.tag}_{name}", num=self.first_sem + len(self.sems)))
        self.sems.append(s)
        return s

    def barrier_and_clear(self):
        nc = self.nc
        first = self.first_sem
        nc.multi_engine_barrier([nc.tensor.engine, nc.vector.engine, nc.scalar.engine, nc.gpsimd.engine,
                                 nc.sync.engine], sems_to_clear=range(first, first + len(self.sems)))


def setup_phase(nc, dram, con, w):
    with ExitStack() as ctx:
        m = Memory(nc, ctx, w["first_sem"], "setup")
        loaded = [m.sem(f"loaded{i}") for i in range(3)]
        cb_scaled, cb_turned, upper_done, done = (m.sem(n) for n in ("cb_scaled", "cb_turned", "upper_done", "done"))
        cb = m.sb("cb", [P, KC, C])
        scb = m.sb("scb", [P, KC])
        full = {n: m.sb(f"full_{n}", [P, KC, 3 * C if n.startswith("qkv") else C])
                for n in ("qkv_a", "proj_a", "qkv_b", "proj_b")}
        turned = m.ps("turned", [P, KC, C])
        def rows(x):
            return x.rearrange("(k p) n -> p k n", p=P)

        def for_all(x):
            return x.rearrange("(o n) -> o n", o=1).broadcast_to([P, C])
        loads = [[(full["qkv_a"][:], rows(dram["w_qkv"])), (w["ident"][:], con["ident"])],
                 [(cb[:], rows(dram["CB"])), (scb[:], dram["SCB"].rearrange("(k p) -> p k", p=P))],
                 [(full["proj_a"][:], rows(dram["w_proj"])),
                  (full["qkv_b"][:, :, 0:C], rows(dram["Wq"])), (full["qkv_b"][:, :, C:2 * C], rows(dram["Wk"])),
                  (full["qkv_b"][:, :, 2 * C:3 * C], rows(dram["Wv"])), (full["proj_b"][:], rows(dram["Wo"])),
                  (w["b_proj"][:], for_all(dram["b_proj"])), (w["b_ffn"][:], for_all(dram["b_ffn"]))]]
        splits = [("qkv_a", full["qkv_a"], 0), ("ffn", turned, None), ("proj_a", full["proj_a"], 2),
                  ("qkv_b", full["qkv_b"], 2), ("proj_b", full["proj_b"], 2)]
        with nc.Block() as block:
            @block.sync
            def _(sp):
                for i, group in enumerate(loads):
                    for dst, src in group:
                        sp.dma_start(dst, src, allow_slow_non_contiguous=True).then_inc(loaded[i], 16)
                for i, group in enumerate(loads):
                    sp.wait_ge(loaded[i], 16 * len(group))

            @block.vector
            def _(dve):
                dve.wait_ge(loaded[1], 16 * len(loads[1]))
                for k in range(KC):
                    dve.tensor_scalar(cb[:, k, :], cb[:, k, :], scb[:, k:k + 1], 1.0 / 127.0,
                                      ALU.mult, ALU.mult).then_inc(cb_scaled, 1)
                dve.wait_ge(loaded[0], 16 * len(loads[0]))
                dve.tensor_copy(w["ident_b"][:], w["ident"][:]).then_inc(done, 1)
                for i, (name, x, _) in enumerate(splits):
                    dve.wait_ge(upper_done, i + 1)
                    dve.tensor_tensor(w[name][:, LOWER], x[:], w[name][:, UPPER], ALU.subtract).then_inc(done, 1)

            @block.scalar
            def _(act):
                for name, x, i in splits:
                    if i is None:
                        act.wait_ge(cb_turned, 1)
                    else:
                        act.wait_ge(loaded[i], 16 * len(loads[i]))
                    act.activation(w[name][:, UPPER], x[:], ACT.Copy).then_inc(upper_done, 1)

            @block.tensor
            def _(pe):
                pe.wait_ge(loaded[0], 16 * len(loads[0]))
                pe.wait_ge(cb_scaled, KC)
                for k in range(KC):
                    for n in range(KC):
                        last = pe.transpose(turned[:, k, n * P:(n + 1) * P], cb[:, n, k * P:(k + 1) * P], w["ident"][:])
                last.then_inc(cb_turned, 1)
        m.barrier_and_clear()


def token_phase(nc, dram, con, w, scr, tag, src, dst, attn, w_proj, b_proj, has_ffn, w_qkv, pos, windows):
    order = {(False, True): [("stat_q", 0), ("turn_q", 1), ("norm_q", 0), ("qkv", 2)],
             (True, True): [("project", 1), ("stat_f", 1), ("scale_a", 0), ("ffn", 3), ("norm_f", 1), ("turn_f", 2),
                            ("stat_q", 3), ("qkv", 5), ("norm_q", 3), ("turn_q", 4)],
             (True, False): [("project", 1), ("stat_f", 1), ("scale_a", 0), ("ffn", 3), ("turn_f", 2), ("norm_f", 1)],
             }[w_proj is not None, w_qkv is not None]
    NGR = BATCHES * QG
    with ExitStack() as ctx:
        m = Memory(nc, ctx, w["first_sem"], tag)
        X = m.sb("X", [P, NGR * TG, C])
        stats = m.sb("stats", [P, TG, 6])
        mv = m.sb("mv", [P, TG, 2])
        var = m.sb("var", [P, TG])
        rstd = m.sb("rstd", [P, TG])
        power = m.sb("power", [P, TG])
        xn = m.sb("xn", [P, 2, TG, C])
        t_bank = [m.ps(f"t_bank{k}", [P, GW]) for k in range(KC)]
        if w_proj is not None:
            y_bank = [m.ps(f"y_bank{k}", [P, 2, C]) for k in range(2)]
        x_in = [m.sem(f"x_in{g}") for g in range(NGR)]
        x_out = m.sem("x_out")
        consts_in, power_set = m.sem("consts_in"), m.sem("power_set")
        stats_done, mv_done, var_done, rstd_done = (m.sem(n) for n in ("stats_done", "mv_done", "var_done", "rstd_done"))
        xn_done, turned, upper_done, halves_done = (m.sem(n) for n in ("xn_done", "turned", "upper_done", "halves_done"))
        y_done, y_added = m.sem("y_done"), m.sem("y_added")
        biased_by = {b: m.sem(f"biased_{b}") for b in ("b_proj", "b_ffn")}
        if w_proj is not None:
            at = m.sb("at", [P, NGR, KC, GW])
            inv = m.sb("inv", [P, INV_RING, KC, GW])
            inv_in = [m.sem(f"inv_in{g}") for g in range(INV_RING)]
            sums_in = [m.sem(f"sums_in{b}") for b in range(B)]
            inverted, inv_out, scaled = m.sem("inverted"), m.sem("inv_out"), m.sem("scaled")
            xT_a = m.sb("xT_a", [P, 2, KC, GW], F32R)
            at_in = [m.sem(f"at_in{g}") for g in range(NGR)]
        if has_ffn:
            xT_f = m.sb("xT_f", [P, 2, KC, GW], F32R)
        if w_qkv is not None:
            xT_q = m.sb("xT_q", [P, 2, 2, KC, GW], F32R)
            R = m.sb("R", [P, RING, GW])
            parts = m.sb("parts", [P, RING, PARTS, GW], BF16)
            v_rows = m.sb("v_rows", [P, RING, 2, H, VW])
            QKB = 2 if w_proj is not None else 4
            if pos:
                F = m.sb("F", [P, RING, GW])
            qk_bank = [m.ps(f"qk_bank{k}", [P, GW]) for k in range(QKB)]
            v_bank = [m.ps(f"v_bank{k}", [P, 2, C]) for k in range(2)]
            qk_done, hi_done, rest_done, mid_done, low_done = (
                m.sem(n) for n in ("qk_done", "hi_done", "rest_done", "mid_done", "low_done"))
            f_done = m.sem("f_done") if pos else qk_done
            bank_read = f_done if pos else rest_done
            full_of = lambda n: F[:, n % RING, :] if pos else qk_bank[n % QKB][:]
            parts_out = [m.sem(f"parts_out{i}") for i in range(RING)]
            v_done, v_copied = m.sem("v_done"), m.sem("v_copied")
            v_out = [m.sem(f"v_out{i}") for i in range(RING)]
            if pos:
                pos_sb = m.sb("pos", [P, S])
            if windows:
                zeros = m.sb("zeros", [PAD, BATCHES * H * VW])
                pads_out = m.sem("pads_out")

        PIECE = H * S // P

        def piece(i, b):
            return at[:, i].rearrange("p k n -> p (k n)")[:, b * PIECE:(b + 1) * PIECE]

        def batch_sums(x, b):
            return x[b * H:(b + 1) * H, :].rearrange("h (x c) -> (h x) c", c=PIECE)

        with nc.Block() as block:
            @block.vector
            def _(dve):
                n = 1
                dve.memset(power[:], -0.5).then_inc(power_set, 1)
                if w_qkv is not None:
                    dve.memset(v_rows[:], 1.0).then_inc(power_set, 1)
                    n += 1
                if windows:
                    dve.memset(zeros[:], 0.0).then_inc(power_set, 1)
                    n += 1
                dve.wait_ge(power_set, n)
                if w_proj is not None:
                    for i in range(B):
                        dve.wait_ge(sums_in[i], 16)
                        dve.reciprocal(piece(1, i), piece(0, i)).then_inc(inverted, 1)
                if pos:
                    dve.wait_ge(consts_in, 16)

            @block.sync
            def _(sp):
                if w_proj is not None:
                    for i in range(B):
                        sp.dma_start(piece(0, i), batch_sums(attn["sums"], i)).then_inc(sums_in[i], 16)
                if pos:
                    sp.dma_start(pos_sb[:], con["pos_t"]).then_inc(consts_in, 16)
                    sp.wait_ge(consts_in, 16)
                if w_proj is not None:
                    for i in range(B):
                        sp.wait_ge(inverted, i + 1)
                        sp.dma_start(batch_sums(attn["inv"], i), piece(1, i)).then_inc(inv_out, 16)
                    sp.wait_ge(inv_out, 16 * B)
        m.barrier_and_clear()

        def slots():
            for t in range(NGR + max(lag for _, lag in order)):
                for stage, lag in order:
                    if 0 <= t - lag < NGR:
                        yield stage, t - lag

        Y = {"project": 2, "ffn": 2}
        TURN = {"scale_a": KC, "turn_f": KC, "turn_q": KC}

        def upto(per, stage, g):
            n = 0
            for s, gg in slots():
                n += per.get(s, 0)
                if (s, gg) == (stage, g):
                    return n

        turns = [(stage, g) for stage, g in slots() if stage in TURN and stage != "scale_a"]
        norm_turned = [KC * (n + 1) for n in range(len(turns))]
        norm_halved = [upto(TURN, *x) for x in turns]

        def halves_of(stage, g):
            if stage == "turn_q":
                return xT_q[:, g % 2]
            return {"scale_a": xT_a if w_proj is not None else None, "turn_f": xT_f if has_ffn else None}[stage][:]

        @contextmanager
        def batches():
            with nc.Fori(0, B // BATCHES) as b:
                with nc.Block() as block:
                    yield b, block
                m.barrier_and_clear()

        with batches() as (b, block):
            @block.sync
            def _(sp):
                def tokens(x, g):
                    return x(b * BATCHES + g // QG)[:, g % QG * TG:(g % QG + 1) * TG, :]

                def batch_of_v(i, n=1):
                    return scr["v"].rearrange("s (b c) -> s b c", b=B)[:, bass.ds(b * BATCHES + i, n), :]

                def load_inv(g):
                    for k in range(KC):
                        src = attn["inv"].rearrange("(b k h) s -> b k h s", b=B, k=KC)[
                            bass.ds(b * BATCHES + g // QG, 1), k, :, g % QG * GW:(g % QG + 1) * GW]
                        sp.dma_start(inv[:, g % INV_RING, k, :],
                                     src.rearrange("o h s -> (o h) s").unsqueeze(1).broadcast_to([H // KC, D, GW])
                                     ).then_inc(inv_in[g % INV_RING], 16)

                for g in range(NGR):
                    if w_proj is not None:
                        cols = slice(g % QG * GW, (g % QG + 1) * GW)
                        sp.dma_start(at[:, g], attn["out"].rearrange("(b k h) d s -> b (h d) k s", b=B, k=KC)[
                            bass.ds(b * BATCHES + g // QG, 1), :, :, cols].rearrange("o p k s -> (o p) k s")
                            ).then_inc(at_in[g], 16)
                        if g < INV_RING:
                            load_inv(g)
                    sp.dma_start(X[:, g * TG:(g + 1) * TG, :], tokens(src, g)).then_inc(x_in[g], 16)
                if windows:
                    for first in (0, PAD + S):
                        sp.dma_start(batch_of_v(0, BATCHES)[first:first + PAD].rearrange("s b c -> s (b c)"),
                                     zeros[:]).then_inc(pads_out, 16)
                n_qk = n_v = n_y = n_out = 0
                last_add = "ffn" if has_ffn else "project"
                for stage, g in slots():
                    if stage == "scale_a" and g + INV_RING < NGR:
                        sp.wait_ge(scaled, g + 1)
                        load_inv(g + INV_RING)
                    if stage in ("project", "ffn"):
                        n_y += 2
                    if dst and stage == last_add:
                        sp.wait_ge(y_added, n_y)
                        sp.dma_start(tokens(dst, g), X[:, g * TG:(g + 1) * TG, :]).then_inc(x_out, 16)
                        n_out += 1
                    if stage == "qkv":
                        for i in range(4):
                            sp.wait_ge(low_done, n_qk + 1)
                            sp.wait_ge(mid_done, n_qk + 1)
                            sp.wait_ge(hi_done, n_qk + 1)
                            sp.dma_start(
                                scr["qk"][i // 2][(b * BATCHES + g // QG) * 2 + i % 2, :, :, :,
                                                  g % QG * GW:(g % QG + 1) * GW].rearrange("h d p s -> (h d) p s"),
                                parts[:, n_qk % RING]).then_inc(parts_out[n_qk % RING], 16)
                            n_qk += 1
                            if i % 2 == 0:
                                continue
                            sp.wait_ge(v_copied, n_v + 1)
                            first = PAD + (g % QG) * GW + i // 2 * 2 * P
                            sp.dma_start(batch_of_v(g // QG)[first:first + 2 * P].rearrange("(u p) o c -> p u (o c)", p=P),
                                         v_rows[:, n_v % RING].rearrange("p u h c -> p u (h c)")
                                         ).then_inc(v_out[n_v % RING], 16)
                            n_v += 1
                if n_out:
                    sp.wait_ge(x_out, 16 * n_out)
                if n_qk:
                    for i in range(RING):
                        sp.wait_ge(parts_out[i], 16 * (n_qk // RING))
                        sp.wait_ge(v_out[i], 16 * (n_v // RING))
                if windows:
                    sp.wait_ge(pads_out, 32)

            @block.vector
            def _(dve):
                n_stat = n_norm = n_turn = n_y = n_qk = 0
                for stage, g in slots():
                    tiles = range(g * TG, (g + 1) * TG)
                    if stage in ("project", "ffn"):
                        if stage == "project" and b_proj is None:
                            dve.wait_ge(x_in[g], 16)
                        else:
                            dve.wait_ge(biased_by[b_proj if stage == "project" else "b_ffn"], g + 1)
                        for i in range(2):
                            t = g * TG + 2 * i
                            dve.wait_ge(y_done, n_y + 1)
                            dve.tensor_tensor(X[:, t:t + 2, :], y_bank[n_y % 2][:], X[:, t:t + 2, :],
                                              ALU.add).then_inc(y_added, 1)
                            n_y += 1
                    if stage in ("stat_f", "stat_q"):
                        if w_proj is None:
                            dve.wait_ge(x_in[g], 16)
                        else:
                            dve.wait_ge(y_added, upto(Y, {"stat_f": "project", "stat_q": "ffn"}[stage], g))
                        if n_stat:
                            dve.wait_ge(mv_done, TG * n_stat)
                        for i, t in enumerate(tiles):
                            dve.bn_stats(stats[:, i, :], X[:, t, :]).then_inc(stats_done, 1)
                        dve.wait_ge(stats_done, TG * (n_stat + 1))
                        if n_stat:
                            dve.wait_ge(xn_done, TG * n_stat)
                            dve.wait_ge(rstd_done, n_stat)
                        for i in range(TG):
                            dve.bn_aggr(mv[:, i, :], stats[:, i, :]).then_inc(mv_done, 1)
                        n_stat += 1
                    if stage in TURN:
                        out = halves_of(stage, g)
                        for k in range(KC):
                            dve.wait_ge(upper_done, n_turn + 1)
                            full = at[:, g, k, :] if stage == "scale_a" else t_bank[k][:]
                            dve.tensor_tensor(out[:, LOWER, k, :], full, out[:, UPPER, k, :],
                                              ALU.subtract).then_inc(halves_done, 1)
                            n_turn += 1
                    if stage in ("norm_f", "norm_q"):
                        dve.wait_ge(rstd_done, n_norm + 1)
                        dve.wait_ge(mv_done, TG * (n_norm + 1))
                        if n_norm >= 2:
                            dve.wait_ge(turned, norm_turned[n_norm - 2])
                        for i, t in enumerate(tiles):
                            dve.tensor_scalar(xn[:, n_norm % 2, i, :], X[:, t, :], mv[:, i, 0:1], rstd[:, i:i + 1],
                                              ALU.subtract, ALU.mult).then_inc(xn_done, 1)
                        n_norm += 1
                    if stage == "qkv":
                        def full(n):
                            dve.wait_ge(qk_done, n + 1)
                            if n >= RING:
                                dve.wait_ge(hi_done, n - RING + 1)
                                dve.wait_ge(rest_done, n - RING + 1)
                            dve.tensor_tensor(F[:, n % RING, :], qk_bank[n % QKB][:], pos_sb[:, g % QG * GW:(g % QG + 1) * GW],
                                              ALU.add).then_inc(f_done, 1)

                        def rest(n):
                            dve.wait_ge(f_done, n + 1)
                            dve.wait_ge(hi_done, n + 1)
                            if n >= RING:
                                dve.wait_ge(mid_done, n - RING + 1)
                                dve.wait_ge(low_done, n - RING + 1)
                            dve.tensor_tensor(R[:, n % RING, :], full_of(n), parts[:, n % RING, 0, :],
                                              ALU.subtract).then_inc(rest_done, 1)
                        for i in range(4):
                            if pos:
                                full(n_qk + i)
                            if i >= 2:
                                rest(n_qk + i - 2)
                        rest(n_qk + 2)
                        rest(n_qk + 3)
                        n_qk += 4

            @block.gpsimd
            def _(pool):
                n_stat = n_norm = n_qk = 0

                def bias(g, b):
                    for t in range(g * TG, (g + 1) * TG):
                        last = pool.tensor_tensor(X[:, t, :], X[:, t, :], w[b][:], ALU.add)
                    last.then_inc(biased_by[b], 1)

                for stage, g in slots():
                    if stage == "project" and b_proj is not None:
                        for x in range(0 if g == 0 else g + 1, min(g + 2, NGR)):
                            pool.wait_ge(x_in[x], 16)
                            bias(x, b_proj)
                    if stage == "scale_a":
                        for x in range(0 if g == 0 else g + 1, min(g + 2, NGR)):
                            pool.wait_ge(at_in[x], 16)
                            pool.wait_ge(inv_in[x % INV_RING], 16 * KC * (x // INV_RING + 1))
                            pool.tensor_tensor(at[:, x], at[:, x], inv[:, x % INV_RING], ALU.mult).then_inc(scaled, 1)
                    if stage in ("stat_f", "stat_q"):
                        pool.wait_ge(mv_done, TG * (n_stat + 1))
                        if n_stat:
                            pool.wait_ge(xn_done, TG * n_stat)
                        pool.tensor_scalar(var[:], mv[:, :, 1], EPS, None, ALU.add).then_inc(var_done, 1)
                        pool.wait_ge(var_done, n_stat + 1)
                        pool.tensor_tensor(rstd[:], var[:], power[:], ALU.pow).then_inc(rstd_done, 1)
                        n_stat += 1
                    if stage in ("norm_f", "norm_q"):
                        n_norm += 1
                        if stage == "norm_f":
                            pool.wait_ge(xn_done, TG * n_norm)
                            bias(g, "b_ffn")
                    if stage == "qkv":
                        for i in range(4):
                            pool.wait_ge(rest_done, n_qk + 1)
                            pool.wait_ge(mid_done, n_qk + 1)
                            if n_qk >= RING:
                                pool.wait_ge(parts_out[n_qk % RING], 16 * (n_qk // RING))
                            pool.tensor_tensor(parts[:, n_qk % RING, 2, :], R[:, n_qk % RING, :], parts[:, n_qk % RING, 1, :],
                                               ALU.subtract).then_inc(low_done, 1)
                            n_qk += 1

            @block.scalar
            def _(act):
                n_turn = n_pe = n_qk = n_v = 0
                for stage, g in slots():
                    if stage in TURN:
                        for k in range(KC):
                            if stage == "scale_a":
                                act.wait_ge(scaled, g + 1)
                                full = at[:, g, k, :]
                            else:
                                act.wait_ge(turned, n_pe + 1)
                                full = t_bank[k][:]
                                n_pe += 1
                            if stage == "scale_a" and g >= 1:
                                act.wait_ge(y_done, upto(Y, "project", g - 1))
                            if stage == "turn_f" and g >= 1:
                                act.wait_ge(y_done, upto(Y, "ffn", g - 1))
                            if stage == "turn_q" and g >= 2:
                                act.wait_ge(qk_done, 4 * (g - 1))
                                act.wait_ge(v_done, TG // 2 * (g - 1))
                            act.activation(halves_of(stage, g)[:, UPPER, k, :], full, ACT.Copy).then_inc(upper_done, 1)
                            n_turn += 1
                    if stage == "qkv":
                        def hi(n):
                            act.wait_ge(f_done, n + 1)
                            if n >= RING:
                                act.wait_ge(parts_out[n % RING], 16 * (n // RING))
                            act.activation(parts[:, n % RING, 0, :], full_of(n), ACT.Copy).then_inc(hi_done, 1)

                        def mid(n):
                            act.wait_ge(rest_done, n + 1)
                            act.activation(parts[:, n % RING, 1, :], R[:, n % RING, :], ACT.Copy).then_inc(mid_done, 1)

                        def values():
                            nonlocal n_v
                            act.wait_ge(v_done, n_v + 1)
                            if n_v >= RING:
                                act.wait_ge(v_out[n_v % RING], 16 * (n_v // RING))
                            act.activation(v_rows[:, n_v % RING, :, :, 0:D],
                                           v_bank[n_v % 2][:].rearrange("p u (h d) -> p u h d", h=H),
                                           ACT.Copy).then_inc(v_copied, 1)
                            n_v += 1
                        for i in range(4):
                            hi(n_qk + i)
                            if i >= 2:
                                mid(n_qk + i - 2)
                            if i % 2:
                                values()
                        mid(n_qk + 2)
                        mid(n_qk + 3)
                        n_qk += 4

            @block.tensor
            def _(pe):
                n_norm = n_y = n_qk = n_v = 0

                def rows_product(bank, xT, first, weights, cols):
                    for i in range(2):
                        for n, (k, x_half, w_half) in enumerate(PRODUCTS):
                            last = pe.matmul(bank[:, i, :], xT[:, x_half, k, first + i * P:first + (i + 1) * P],
                                             weights[:, w_half, k, cols], start=(n == 0), stop=(n == len(PRODUCTS) - 1))
                    return last

                for stage, g in slots():
                    if stage in ("project", "ffn"):
                        turn, weights = ("scale_a", w[w_proj]) if stage == "project" else ("turn_f", w["ffn"])
                        pe.wait_ge(halves_done, upto(TURN, turn, g))
                        for i in range(2):
                            if n_y >= 2:
                                pe.wait_ge(y_added, n_y - 1)
                            rows_product(y_bank[n_y % 2], halves_of(turn, g), 2 * i * P, weights,
                                         slice(0, C)).then_inc(y_done, 1)
                            n_y += 1
                    if stage in ("turn_f", "turn_q"):
                        pe.wait_ge(xn_done, TG * (n_norm + 1))
                        if n_norm:
                            pe.wait_ge(halves_done, norm_halved[n_norm - 1])
                        for k in range(KC):
                            for i in range(TG):
                                last = pe.transpose(t_bank[k][:, i * P:(i + 1) * P],
                                                    xn[:, n_norm % 2, i, k * P:(k + 1) * P], w["ident"][:])
                            last.then_inc(turned, 1)
                        n_norm += 1
                    if stage == "qkv":
                        pe.wait_ge(halves_done, upto(TURN, "turn_q", g))
                        xT = halves_of("turn_q", g)
                        for i in range(4):
                            if n_qk >= QKB:
                                pe.wait_ge(bank_read, n_qk - QKB + 1)
                            for n, (k, x_half, w_half) in enumerate(PRODUCTS):
                                last = pe.matmul(qk_bank[n_qk % QKB][:], w[w_qkv][:, w_half, k, i * P:(i + 1) * P],
                                                 xT[:, x_half, k, :], start=(n == 0), stop=(n == len(PRODUCTS) - 1))
                            last.then_inc(qk_done, 1)
                            n_qk += 1
                            if i % 2:
                                if n_v >= 2:
                                    pe.wait_ge(v_copied, n_v - 1)
                                rows_product(v_bank[n_v % 2], xT, i // 2 * 2 * P, w[w_qkv],
                                             slice(2 * C, 3 * C)).then_inc(v_done, 1)
                                n_v += 1


def attention_phase(nc, con, w, scr, tag, windows, score_scale):
    KW = P + 2 * WIN
    QT = NT
    if windows:
        units = [(g, None, None, 0) for g in range(QG)]
    else:
        units = []
        for g in range(QG):
            full, diag = list(range(TG * g)), list(range(TG * g, TG * (g + 1)))
            if full:
                diag.append(diag.pop(0))
            for i in range(max(len(full), TG)):
                units += [(g, kb, kb, max(0, kb - TG * g) * P) for x in (full, diag) for kb in x[i:i + 1]]
    U = len(units)
    last_unit = {g: max(u for u in range(U) if units[u][0] == g) for g in range(QG)}
    if windows:
        jobs = [(g, j, t, 0, 2 * KW) for g in range(QG) for t in range(g * TG, (g + 1) * TG, 2) for j in range(HG)]
    else:
        jobs = [(t // TG, j, t, c, min(GW, (t + 1) * P - c * GW))
                for t in range(QT) for j in range(HG) for c in range(t // TG + 1)]
    weight = [sum(GW - x[3] for x in units[:u + 1]) for u in range(U)]
    cols = [sum(x[4] for x in jobs[:i + 1]) for i in range(len(jobs))]
    unit_of = [min(u for u in range(U) if cols[i] * weight[-1] <= weight[u] * cols[-1] + 1) for i in range(len(jobs))]
    jobs_at = [[i for i in range(len(jobs)) if unit_of[i] == u] for u in range(U)]
    group_jobs = [sum(1 for x in jobs if x[0] <= g) for g in range(QG)]
    turn_at = [unit_of[group_jobs[g] - 1] + (1 if windows else 2) for g in range(QG)]

    with ExitStack() as ctx:
        m = Memory(nc, ctx, w["first_sem"], tag)
        QA = m.sb("QA", [P, BUFS, HG, SP_], BF16)
        KA = m.sb("KA", [P, BUFS, HG, SP_], BF16)
        VT = NW if windows else NT
        V_LOADS = VT // NT
        OUTS = HG + 1
        V = m.sb("V", [P, BUFS, VT, HG, VW])
        probs = m.sb("probs", [P, 2, HG, GW])
        o_sb = m.sb("o_sb", [P, 2, 2 * GW])
        part = m.sb("part", [P, HG, QT, QG])
        top = m.sb("top", [P, 2, HG, TG])
        neg = m.sb("neg", [P, HG, TG])
        rest = m.sb("rest", [P, HG, TG])
        top_parts = m.sb("top_parts", [P, 2, PARTS, HG, TG], BF16)
        low = m.sb("low", [PARTS * HG * TG, LOWS, P], BF16)
        if windows:
            mask_f = probs[:, 0, 0:3, :].rearrange("p a n -> p (a n)")
            mask_k = m.sb("mask_k", [P, 3, GW], BF16)
            mask_q = m.sb("mask_q", [P, 3, 2 * KW])
        else:
            mask_f = probs[:, 0, 0, 0:P]
            mask_k = m.sb("mask_k", [P, P], BF16)
            mask_q = m.sb("mask_q", [P, GW])
        junk = m.sb("junk", [P, 2, GW], BF16)
        ones = m.sb("ones", [PARTS, S], BF16)
        s_bank = m.ps("s_bank", [P, 2, 2, GW])
        m_bank = [m.ps(f"m_bank{i}", [P, GW]) for i in range(M_RING)]
        o_bank = m.ps("o_bank", [P, GW])

        setup, set_in, pads_set = m.sem("setup"), m.sem("set_in"), m.sem("pads_set")
        ones_set, ones_in = m.sem("ones_set"), m.sem("ones_in")
        qk_in = [m.sem(f"qk_in{k}") for k in range(BUFS)]
        v_in = [m.sem(f"v_in{k}") for k in range(BUFS)]
        low_kept = [m.sem(f"low_kept{i}") for i in range(LOWS)]
        low_in = [[m.sem(f"low_in{k}{g}") for g in range(QG)] for k in range(BUFS)]
        out_done = [m.sem(f"out_done{i}") for i in range(2)]
        s_done, exp_done, pv_done = m.sem("s_done"), m.sem("exp_done"), m.sem("pv_done")
        m_done, m_free, top_done = m.sem("m_done"), m.sem("m_free"), m.sem("top_done")
        neg_done, split_1, split_2, split_3, split_4, top_turned, low_done = (
            m.sem(n) for n in ("neg_done", "split_1", "split_2", "split_3", "split_4", "top_turned", "low_done"))
        o_copied = m.sem("o_copied")

        def load(sp, step, buf, arrived, operands=(0, 1)):
            for which in operands:
                blocks, dst = ((Q_BLOCKS, QA), (K_BLOCKS, KA))[which]
                for i, part in enumerate(blocks):
                    src = scr["qk"][which].rearrange("o h d p s -> (o h) d p s")[bass.ds(step * HG, HG), :, part, :]
                    sp.dma_start(dst[i * D:(i + 1) * D, buf, :, PAD:PAD + S],
                                 src.rearrange("j d s -> d j s")).then_inc(arrived, 16)

        def load_v(sp, step, buf, arrived):
            src = scr["v"].rearrange("s (t c) -> t s c", t=STEPS)[bass.ds(step, 1)]
            for i, first in enumerate((0, WQ) if windows else (PAD,)):
                dst = V[:, buf, i:VT:2] if windows else V[:, buf]
                sp.dma_start(dst.rearrange("p u j c -> p u (j c)"),
                             src[:, first:first + S].rearrange("o (u p) c -> p (o u) c", p=P)).then_inc(arrived, 16)

        with nc.Block() as block:
            @block.sync
            def _(sp):
                load(sp, 0, 0, qk_in[0])
                if windows:
                    sp.dma_start(mask_f, con["win_k"]).then_inc(set_in, 16)
                    sp.dma_start(mask_q[:].rearrange("p a n -> p (a n)"), con["win_q"]).then_inc(set_in, 16)
                else:
                    sp.dma_start(mask_f, con["causal_kq"]).then_inc(set_in, 16)
                    sp.dma_start(mask_q[:], con["causal_q"]).then_inc(set_in, 16)
                sp.wait_ge(ones_set, 1)
                for j in range(HG):
                    sp.dma_start(KA[ROWS:ROWS + PARTS, :, j, PAD:PAD + S],
                                 ones[:].unsqueeze(1).broadcast_to([PARTS, BUFS, S])).then_inc(ones_in, 16)
                sp.wait_ge(set_in, 32)
                sp.wait_ge(ones_in, 16 * HG)
                sp.wait_ge(qk_in[0], 16 * ROW_LOADS)

            @block.vector
            def _(dve):
                dve.memset(part[:], LOWEST).then_inc(setup, 1)
                dve.memset(o_bank[:], 0.0).then_inc(setup, 1)
                dve.wait_ge(set_in, 32)
                dve.tensor_copy(mask_k[:].rearrange("p a n -> p (a n)") if windows else mask_k[:],
                                mask_f).then_inc(setup, 1)
                dve.wait_ge(setup, 3)

            @block.gpsimd
            def _(pool):
                pool.memset(ones[:], 1.0).then_inc(ones_set, 1)
                for X in (QA, KA):
                    pool.memset(X[:, :, :, 0:PAD], 0.0).then_inc(pads_set, 1)
                    pool.memset(X[:, :, :, PAD + S:SP_], 0.0).then_inc(pads_set, 1)
                pool.wait_ge(pads_set, 4)
        m.barrier_and_clear()

        def part_of_program(steps, loads, block, exp=True, maximum=True):
            K = len(steps)
            max_buf = [(k + (1 if exp else 0)) % BUFS for k in range(K)]

            def slots():
                return [(n, n // U, n % U) for n in range(K * U + 2)]

            def turned_in(n):
                return [(k, g) for k in range(K) for g in range(QG) if maximum and k * U + turn_at[g] == n]

            def copied_in(n):
                return [(k, g) for k in range(K) for g in range(QG) if exp and k * U + last_unit[g] + 1 == n]

            order = []
            for n, k, u in slots():
                todo = [(k, "job", i) for i in jobs_at[u]] if k < K and maximum else []
                after = min(2, (len(todo) + 1) // 2) if exp else 0
                before = len(todo) - after
                if exp and k < K:
                    order.append((k, "scores", (u, 0)))
                order += todo[:(before + 1) // 2]
                if exp and k < K:
                    order.append((k, "scores", (u, 1)))
                order += todo[(before + 1) // 2:before]
                if exp and 1 <= n <= K * U:
                    order.append(((n - 1) // U, "values", (n - 1) % U))
                order += todo[before:]
                order += [(k, "turn_top", g) for k, g in turned_in(n)]
            ring = [x for x in order if x[1] in ("job", "turn_top")]
            place = {x: n for n, x in enumerate(ring)}

            def bank_of(*use):
                return m_bank[place[use] % M_RING]

            def wait_bank(pe, *use):
                n = place[use] - M_RING
                if n >= 0:
                    what = ring[n][1]
                    reads = {"job": m_free, "turn_top": low_done}[what]
                    pe.wait_ge(reads, sum(1 for x in ring[:n + 1] if x[1] == what))

            @block.sync
            def _(sp):
                n_low = 0

                def fetch(n):
                    k, g = n // QG, n % QG
                    sp.wait_ge(low_kept[n % LOWS], 16 * (n // LOWS + 1))
                    sp.dma_start(QA[ROWS:ROWS + PARTS, max_buf[k], :, PAD + g * GW:PAD + (g + 1) * GW],
                                 scr["low"][n]).then_inc(low_in[k][g], 16)

                for n, k, u in slots():
                    if k < K and loads[k] is not None:
                        if u == 0 and exp and k:
                            sp.wait_ge(s_done, 2 * k * U)
                            if k >= 2:
                                sp.wait_ge(pv_done, (k - 1) * U)
                        (qk_step, qk_buf), (v_step, v_buf) = loads[k]
                        if u < 2:
                            load(sp, qk_step, qk_buf, qk_in[k], operands=(u,))
                        if u == 2:
                            load_v(sp, v_step, v_buf, v_in[k])
                    for _ in turned_in(n):
                        sp.wait_ge(low_done, n_low + 1)
                        sp.dma_start(scr["low"][n_low].rearrange("r j (t q) -> (r j t) q", t=TG),
                                     low[:, n_low % LOWS, :]).then_inc(low_kept[n_low % LOWS], 16)
                        if n_low:
                            fetch(n_low - 1)
                        n_low += 1
                    for k, g in copied_in(n):
                        if g % 2:
                            sp.wait_ge(o_copied, k * QG + g + 1)
                            cols = slice((g - 1) * GW, (g + 1) * GW)
                            half = g // 2
                            for j in range(HG):
                                sp.dma_start(scr["out"].rearrange("(s j) d n -> s j d n", j=HG)[
                                    bass.ds(steps[k], 1), j, :, cols].rearrange("o d n -> (o d) n"),
                                    o_sb[32 * j:32 * j + D, half, :]).then_inc(out_done[half], 16)
                            sp.dma_start(scr["sums"][bass.ds(steps[k] * HG, HG), cols],
                                         o_sb[D:P:32, half, :]).then_inc(out_done[half], 16)
                if n_low:
                    fetch(n_low - 1)
                for k in range(K):
                    if loads[k] is not None:
                        sp.wait_ge(qk_in[k], 16 * ROW_LOADS)
                        sp.wait_ge(v_in[k], 16 * V_LOADS)
                    if maximum:
                        for g in range(QG):
                            sp.wait_ge(low_in[k][g], 16)
                if exp:
                    for i in range(2):
                        sp.wait_ge(out_done[i], 16 * OUTS * K)

            @block.tensor
            def _(pe):
                n_half = n_pv = 0

                def scores(k, u, half):
                    nonlocal n_half
                    g, kb, _, off = units[u]
                    buf = k
                    if half == 0 and k and u == last_unit.get(g - 1, -1) + 1:
                        pe.wait_ge(low_in[k - 1][g], 16)
                    if n_half >= 2:
                        pe.wait_ge(exp_done, n_half - 1)
                    for i in range(2):
                        j = 2 * half + i
                        bank = s_bank[:, n_half % 2, i, :]
                        if windows:
                            v = 0 if g == 0 else 2 if g == QG - 1 else 1
                            pe.matmul(bank, w["ident_b"][:], mask_k[:, v, :], start=True, stop=False)
                            for n in range(GW // WQ):
                                q0 = g * GW + n * WQ
                                last = pe.matmul(bank[:, n * WQ:(n + 1) * WQ], KA[0:ROWS + PARTS, buf, j, q0:q0 + P],
                                                 QA[0:ROWS + PARTS, buf, j, PAD + q0:PAD + q0 + WQ],
                                                 start=False, stop=(n == GW // WQ - 1))
                        else:
                            diag = kb >= TG * g
                            last = pe.matmul(bank[:, off:GW], KA[0:ROWS + PARTS, buf, j, PAD + kb * P:PAD + (kb + 1) * P],
                                             QA[0:ROWS + PARTS, buf, j, PAD + g * GW + off:PAD + (g + 1) * GW],
                                             start=True, stop=not diag)
                            if diag:
                                last = pe.matmul(bank[:, off:off + P], w["ident_b"][:], mask_k[:],
                                                 start=False, stop=True)
                    last.then_inc(s_done, 1)
                    n_half += 1

                def values(k, u):
                    nonlocal n_pv
                    g, kb, _, off = units[u]
                    buf = k
                    pe.wait_ge(exp_done, 2 * n_pv + 2)
                    if u == 0 and k:
                        pe.wait_ge(v_in[k - 1], 16 * V_LOADS)
                    first = u == last_unit.get(g - 1, -1) + 1
                    if first and k * QG + g:
                        pe.wait_ge(o_copied, k * QG + g)
                    if windows:
                        for n in range(GW // WQ):
                            for j in range(HG):
                                last = pe.matmul(o_bank[32 * j:32 * j + VW, n * WQ:(n + 1) * WQ],
                                                 V[:, buf, g * (GW // WQ) + n, j, :],
                                                 probs[:, n_pv % 2, j, n * WQ:(n + 1) * WQ], start=True, stop=True)
                    else:
                        for j in range(HG):
                            last = pe.matmul(o_bank[32 * j:32 * j + VW, off:GW], V[:, buf, kb, j, :],
                                             probs[:, n_pv % 2, j, off:GW], start=first, stop=(u == last_unit[g]))
                    last.then_inc(pv_done, 1)
                    n_pv += 1

                def maxima(k, i):
                    g, j, t, c, n = jobs[i]
                    buf = max_buf[k]
                    wait_bank(pe, k, "job", i)
                    bank = bank_of(k, "job", i)
                    q_tile = lambda t: QA[0:ROWS, buf, j, PAD + t * P:PAD + (t + 1) * P]
                    if windows:
                        for x in range(2):
                            last = pe.matmul(bank[:, x * KW:(x + 1) * KW], q_tile(t + x),
                                             KA[0:ROWS, buf, j, (t + x) * P:(t + x) * P + KW], start=True, stop=True)
                    else:
                        last = pe.matmul(bank[:, 0:n], q_tile(t), KA[0:ROWS, buf, j, PAD + c * GW:PAD + c * GW + n],
                                         start=True, stop=True)
                    last.then_inc(m_done, 1)

                for k, what, x in order:
                    if what == "scores":
                        if x == (0, 0) and k and maximum:
                            pe.wait_ge(qk_in[k - 1], 16 * ROW_LOADS)
                        scores(k, *x)
                    elif what == "values":
                        values(k, x)
                    elif what == "job":
                        maxima(k, x)
                    else:
                        wait_bank(pe, k, what, x)
                        n = k * QG + x
                        pe.wait_ge(split_4, n + 1)
                        pe.matmul(bank_of(k, what, x)[0:PARTS * HG * TG, 0:P],
                                  top_parts[:, n % 2].rearrange("p r j t -> p (r j t)"), w["ident_b"][:],
                                  start=True, stop=True).then_inc(top_turned, 1)

            @block.scalar
            def _(act):
                n_half = n_pv = 0
                for slot, k, u in slots():
                    if exp and k < K:
                        off = units[u][3]
                        for half in range(2):
                            act.wait_ge(s_done, n_half + 1)
                            if n_pv >= 2 and half == 0:
                                act.wait_ge(pv_done, n_pv - 1)
                            act.activation(probs[:, n_pv % 2, 2 * half:2 * half + 2, off:GW],
                                           s_bank[:, n_half % 2, :, off:GW], ACT.Exp,
                                           scale=score_scale).then_inc(exp_done, 1)
                            n_half += 1
                        n_pv += 1
                    for k, g in copied_in(slot):
                        n = k * QG + g
                        act.wait_ge(pv_done, k * U + last_unit[g] + 1)
                        if n >= 4:
                            act.wait_ge(out_done[n // 2 % 2], 16 * OUTS * (n // 4))
                        act.activation(o_sb[:, n // 2 % 2, n % 2 * GW:(n % 2 + 1) * GW], o_bank[:],
                                       ACT.Copy).then_inc(o_copied, 1)
                    for k, g in turned_in(slot):
                        n = k * QG + g
                        act.wait_ge(top_turned, n + 1)
                        if n >= LOWS:
                            act.wait_ge(low_kept[n % LOWS], 16 * (n // LOWS))
                        act.activation(low[:, n % LOWS, :], bank_of(k, "turn_top", g)[0:PARTS * HG * TG, 0:P],
                                       ACT.Copy).then_inc(low_done, 1)

            @block.vector
            def _(dve):
                n_job = n_top = 0

                for k in range(K):
                    for u in range(U):
                        if maximum:
                            for i in jobs_at[u]:
                                g, j, t, c, n = jobs[i]
                                bank = bank_of(k, "job", i)
                                dve.wait_ge(m_done, n_job + 1)
                                if windows:
                                    v = 0 if t == 0 else 2 if t == QT - 2 else 1
                                    if n_job >= 2:
                                        dve.wait_ge(m_free, n_job - 1)
                                    for x in range(2):
                                        ins = dve.tensor_tensor_reduce(
                                            junk[:, n_job % 2, x * KW:(x + 1) * KW], bank[:, x * KW:(x + 1) * KW],
                                            mask_q[:, v, x * KW:(x + 1) * KW], 1.0, LOWEST, ALU.add, ALU.max,
                                            part[:, j, t + x, 0:1])
                                elif c == t // TG:
                                    if n_job >= 2:
                                        dve.wait_ge(m_free, n_job - 1)
                                    ins = dve.tensor_tensor_reduce(junk[:, n_job % 2, 0:n], bank[:, 0:n], mask_q[:, GW - n:GW], 1.0,
                                                                   LOWEST, ALU.add, ALU.max, part[:, j, t, c:c + 1])
                                else:
                                    ins = dve.tensor_reduce(part[:, j, t, c:c + 1], bank[:, 0:n], AX, ALU.max)
                                ins.then_inc(m_free, 1)
                                n_job += 1
                                if group_jobs[g] == i + 1:
                                    dve.wait_ge(m_free, n_job)
                                    if n_top >= 2:
                                        dve.wait_ge(neg_done, n_top - 1)
                                    dve.tensor_reduce(top[:, n_top % 2], part[:, :, g * TG:(g + 1) * TG, :], AX,
                                                      ALU.max).then_inc(top_done, 1)
                                    n_top += 1

            @block.gpsimd
            def _(pool):
                for n in range(QG * K if maximum else 0):
                    half = top_parts[:, n % 2]
                    pool.wait_ge(top_done, n + 1)
                    if n >= 2:
                        pool.wait_ge(top_turned, n - 1)
                    if n:
                        pool.wait_ge(split_2, n)
                        pool.wait_ge(split_4, n)
                    pool.tensor_scalar(neg[:], top[:, n % 2], -1.0, None, ALU.mult).then_inc(neg_done, 1)
                    pool.wait_ge(neg_done, n + 1)
                    pool.tensor_copy(half[:, 0], neg[:]).then_inc(split_1, 1)
                    pool.wait_ge(split_1, n + 1)
                    pool.tensor_tensor(rest[:], neg[:], half[:, 0], ALU.subtract).then_inc(split_2, 1)
                    pool.wait_ge(split_2, n + 1)
                    pool.tensor_copy(half[:, 1], rest[:]).then_inc(split_3, 1)
                    pool.wait_ge(split_3, n + 1)
                    pool.tensor_tensor(half[:, 2], rest[:], half[:, 1], ALU.subtract).then_inc(split_4, 1)

        with nc.Block() as block:
            part_of_program([0], [((1, 1), (0, 0))], block, exp=False)
        m.barrier_and_clear()
        with nc.Fori(0, LOOPS) as i:
            with nc.Block() as block:
                part_of_program([BUFS * i + k for k in range(BUFS)],
                                [(((BUFS * i + k + 2) % STEPS, (k + 2) % BUFS), (BUFS * i + k + 1, (k + 1) % BUFS))
                                 for k in range(BUFS)], block)
            m.barrier_and_clear()
        with nc.Block() as block:
            part_of_program([STEPS - 1], [None], block, maximum=False)
        m.barrier_and_clear()


def program(nc, dram, con, out):
    with ExitStack() as ctx:
        def sb(name, shape, dt=F32):
            return ctx.enter_context(nc.sbuf_tensor(name, shape, dt))
        with nc.semaphore("lowest_free") as lowest:
            first_sem = lowest.num
        w = {"first_sem": first_sem, **{n: sb(n, [P, 2, KC, 3 * C], F32R) for n in ("qkv_a", "qkv_b")},
             **{n: sb(n, [P, 2, KC, C], F32R) for n in ("proj_a", "proj_b", "ffn")},
             "b_proj": sb("b_proj", [P, C]), "b_ffn": sb("b_ffn", [P, C]),
             "ident": sb("ident", [P, P]), "ident_b": sb("ident_b", [P, P], BF16)}
        x2 = nc.dram_tensor("x2", (B, S, C), F32, kind="Internal").ap()
        qk = [nc.dram_tensor(n, (B * 2, H // 2, D, PARTS, S), BF16, kind="Internal").ap() for n in ("q_parts", "k_parts")]
        v = nc.dram_tensor("values", (SP_, B * H * VW), F32, kind="Internal").ap()
        low = nc.dram_tensor("low_maxima", (BUFS * QG, PARTS, HG, GW), BF16, kind="Internal").ap()
        attn = {"out": nc.dram_tensor("attn_out", (B * H, D, S), F32, kind="Internal").ap(),
                **{n: nc.dram_tensor(f"attn_{n}", (B * H, S), F32, kind="Internal").ap() for n in ("sums", "inv")}}

        def rows(x):
            return lambda b: x[bass.ds(b, 1)].rearrange("o (t p) c -> p (o t) c", p=P)

        setup_phase(nc, dram, con, w)
        token_phase(nc, dram, con, w, {"qk": qk, "v": v}, "first", rows(dram["x"]), None, None, None, None, False,
                    "qkv_a", False, True)
        attention_phase(nc, con, w, {"qk": qk, "v": v, **attn, "low": low}, "window", True, D ** -0.5)
        token_phase(nc, dram, con, w, {"qk": qk, "v": v}, "middle", rows(dram["x"]), rows(x2), attn, "proj_a", "b_proj",
                    True, "qkv_b", True, False)
        attention_phase(nc, con, w, {"qk": qk, "v": v, **attn, "low": low}, "causal", False, C ** -0.5)
        token_phase(nc, dram, con, w, None, "last", rows(x2), rows(out), attn, "proj_b", None, True, None, False, False)


_INS = {"x": "L0_attn_a_x", "w_qkv": "L0_attn_a_w_qkv", "w_proj": "L0_attn_a_w_proj", "b_proj": "L0_attn_a_b_proj",
        "Wq": "L0_attn_b_Wq", "Wk": "L0_attn_b_Wk", "Wv": "L0_attn_b_Wv", "Wo": "L0_attn_b_Wo",
        "CB": "L0_ffn_CB", "SCB": "L0_ffn_SCB", "b_ffn": "L0_ffn_bias"}


def kernel(**inputs):
    import numpy as _np
    import concourse.bacc as _bacc
    from concourse import mybir as _mybir
    from concourse.bass_utils import run_bass_kernel_spmd as _run

    nc = _bacc.Bacc("TRN2", target_bir_lowering=False, num_devices=1)
    arrays, dram, con = {}, {}, {}
    for short, name in _INS.items():
        a = _np.ascontiguousarray(inputs[name])
        arrays[f"in_{short}"] = a
        dram[short] = nc.dram_tensor(f"in_{short}", a.shape, _mybir.dt.from_np(a.dtype), kind="ExternalInput").ap()
    for name, a in constants().items():
        arrays[f"const_{name}"] = a
        con[name] = nc.dram_tensor(f"const_{name}", a.shape, _mybir.dt.from_np(a.dtype), kind="ExternalInput").ap()
    out = nc.dram_tensor("out_dram", (B, S, C), F32, kind="ExternalOutput").ap()
    program(nc, dram, con, out)
    r = _run(nc, [arrays], core_ids=[0])
    return r.results[0]["out_dram"]
```
